# Optimizing a Trainium2 kernel written in Bass

```python
import numpy as np
import jax
import jax.numpy as jnp

def _softmax(x, axis=-1):
    return jax.nn.softmax(x, axis=axis)

def _gelu(x):
    return jax.nn.gelu(x, approximate=True)

def _silu(x):
    return jax.nn.silu(x)

def _sigmoid(x):
    return jax.nn.sigmoid(x)

def _layernorm(x, axis=-1, eps=1e-05):
    m = jnp.mean(x, axis=axis, keepdims=True)
    v = jnp.var(x, axis=axis, keepdims=True)
    return (x - m) / jnp.sqrt(v + eps)

def _scatter_add(tgt, idx, src, axis=0):
    return tgt.at[idx].add(src)

def _segment_sum(src, seg, n):
    return jax.ops.segment_sum(src, seg, n)
kernel_name = 'mk_recurrent_d1_jaxref_r8_4fe92c'

def setup_inputs(seed: int=0):
    np.random.seed(seed)
    _w = jnp.asarray

    def _L0_attn_setup():
        import jax, jax.numpy as jnp
        import numpy as np
        GAMMA = 0.99
        CAUSAL = False
        EPS = 1e-05

        def _ln(x, w, b):
            mu = jnp.mean(x, axis=-1, keepdims=True)
            var = jnp.var(x, axis=-1, keepdims=True)
            return (x - mu) * jax.lax.rsqrt(var + EPS) * w + b

        def _rpe(pos, rpe_pos_w, rpe_ln_w, rpe_ln_b, rpe_fc_w, rpe_out_ln_w, rpe_out_ln_b, rpe_out_w):
            h = pos @ rpe_pos_w
            for i in range(rpe_fc_w.shape[0]):
                h = jax.nn.silu(_ln(h, rpe_ln_w[i], rpe_ln_b[i])) @ rpe_fc_w[i]
            return jax.nn.silu(_ln(h, rpe_out_ln_w, rpe_out_ln_b)) @ rpe_out_w

        def _tno(v, rpe_params):
            b, n, d = v.shape
            idx = jnp.arange(1, n, dtype=v.dtype)[:, None]
            t_zero = _rpe(jnp.zeros((1, 1), v.dtype), *rpe_params)
            t_pos = _rpe(idx, *rpe_params) * GAMMA ** idx
            if CAUSAL:
                t_neg = jnp.zeros((n - 1, d), v.dtype)
            else:
                neg_idx = -idx[::-1]
                t_neg = _rpe(neg_idx, *rpe_params) * GAMMA ** (-neg_idx)
            a = jnp.concatenate([t_zero, t_pos, jnp.zeros((1, d), v.dtype), t_neg], axis=0)
            m = 2 * n
            y = jnp.fft.irfft(jnp.fft.rfft(a, n=m, axis=0)[None] * jnp.fft.rfft(v, n=m, axis=1), n=m, axis=1)
            return y[:, :n].astype(v.dtype)
        key = jax.random.key(seed)
        ks = jax.random.split(key, 6)
        B, N, D, F, L = (4, 256, 128, 32, 3)
        d1 = D
        s = 0.02
        return {'x': jax.random.normal(ks[0], (B, N, D), jnp.float32), 'uv_w': jax.random.normal(ks[1], (D, 2 * d1), jnp.float32) * s, 'o_w': jax.random.normal(ks[2], (d1, D), jnp.float32) * s, 'rpe_pos_w': jax.random.normal(ks[3], (1, F), jnp.float32), 'rpe_ln_w': jnp.ones((L, F), jnp.float32), 'rpe_ln_b': jnp.zeros((L, F), jnp.float32), 'rpe_fc_w': jax.random.normal(ks[4], (L, F, F), jnp.float32) * 0.2, 'rpe_out_ln_w': jnp.ones((F,), jnp.float32), 'rpe_out_ln_b': jnp.zeros((F,), jnp.float32), 'rpe_out_w': jax.random.normal(ks[5], (F, d1), jnp.float32) * 0.1}
    _L0_attn_in = _L0_attn_setup()

    def _L0_ffn_setup():
        import jax, jax.numpy as jnp
        import numpy as np
        B, S, D, F, E, TOP_K = (4, 256, 128, 512, 8, 2)
        LN_EPS = 1e-05
        key = jax.random.key(seed)
        ks = jax.random.split(key, 4)
        sc = lambda fan_in: 1.0 / np.sqrt(fan_in)
        return {'x': jax.random.normal(ks[0], (B, S, D), jnp.float32), 'W1': jax.random.normal(ks[1], (E, D, F), jnp.float32) * sc(D), 'b1': jnp.zeros((E, F), jnp.float32), 'W2': jax.random.normal(ks[2], (E, F, D), jnp.float32) * sc(F), 'b2': jnp.zeros((E, D), jnp.float32), 'Wr': jax.random.normal(ks[3], (D, E), jnp.float32) * sc(D), 'br': jnp.zeros((E,), jnp.float32), 'gamma': jnp.ones((D,), jnp.float32), 'beta': jnp.zeros((D,), jnp.float32)}
    _L0_ffn_in = _L0_ffn_setup()
    _d = {'L0_attn_x': _L0_attn_in['x'], 'L0_attn_uv_w': _L0_attn_in['uv_w'], 'L0_attn_o_w': _L0_attn_in['o_w'], 'L0_attn_rpe_pos_w': _L0_attn_in['rpe_pos_w'], 'L0_attn_rpe_ln_w': _L0_attn_in['rpe_ln_w'], 'L0_attn_rpe_ln_b': _L0_attn_in['rpe_ln_b'], 'L0_attn_rpe_fc_w': _L0_attn_in['rpe_fc_w'], 'L0_attn_rpe_out_ln_w': _L0_attn_in['rpe_out_ln_w'], 'L0_attn_rpe_out_ln_b': _L0_attn_in['rpe_out_ln_b'], 'L0_attn_rpe_out_w': _L0_attn_in['rpe_out_w'], 'L0_ffn_W1': _L0_ffn_in['W1'], 'L0_ffn_b1': _L0_ffn_in['b1'], 'L0_ffn_W2': _L0_ffn_in['W2'], 'L0_ffn_b2': _L0_ffn_in['b2'], 'L0_ffn_Wr': _L0_ffn_in['Wr'], 'L0_ffn_br': _L0_ffn_in['br'], 'L0_ffn_gamma': _L0_ffn_in['gamma'], 'L0_ffn_beta': _L0_ffn_in['beta']}
    _x0 = _d['L0_attn_x']
    _d['L0_attn_x'] = jax.random.normal(jax.random.fold_in(jax.random.key(seed), 1), (8, 512, 128), dtype=_x0.dtype)
    del _x0
    return _d

def reference(L0_attn_x, L0_attn_uv_w, L0_attn_o_w, L0_attn_rpe_pos_w, L0_attn_rpe_ln_w, L0_attn_rpe_ln_b, L0_attn_rpe_fc_w, L0_attn_rpe_out_ln_w, L0_attn_rpe_out_ln_b, L0_attn_rpe_out_w, L0_ffn_W1, L0_ffn_b1, L0_ffn_W2, L0_ffn_b2, L0_ffn_Wr, L0_ffn_br, L0_ffn_gamma, L0_ffn_beta):

    def _L0_attn_ref(x, uv_w, o_w, rpe_pos_w, rpe_ln_w, rpe_ln_b, rpe_fc_w, rpe_out_ln_w, rpe_out_ln_b, rpe_out_w):
        import jax, jax.numpy as jnp
        import numpy as np
        GAMMA = 0.99
        CAUSAL = False
        EPS = 1e-05

        def _ln(x, w, b):
            mu = jnp.mean(x, axis=-1, keepdims=True)
            var = jnp.var(x, axis=-1, keepdims=True)
            return (x - mu) * jax.lax.rsqrt(var + EPS) * w + b

        def _rpe(pos, rpe_pos_w, rpe_ln_w, rpe_ln_b, rpe_fc_w, rpe_out_ln_w, rpe_out_ln_b, rpe_out_w):
            h = pos @ rpe_pos_w
            for i in range(rpe_fc_w.shape[0]):
                h = jax.nn.silu(_ln(h, rpe_ln_w[i], rpe_ln_b[i])) @ rpe_fc_w[i]
            return jax.nn.silu(_ln(h, rpe_out_ln_w, rpe_out_ln_b)) @ rpe_out_w

        def _tno(v, rpe_params):
            b, n, d = v.shape
            idx = jnp.arange(1, n, dtype=v.dtype)[:, None]
            t_zero = _rpe(jnp.zeros((1, 1), v.dtype), *rpe_params)
            t_pos = _rpe(idx, *rpe_params) * GAMMA ** idx
            if CAUSAL:
                t_neg = jnp.zeros((n - 1, d), v.dtype)
            else:
                neg_idx = -idx[::-1]
                t_neg = _rpe(neg_idx, *rpe_params) * GAMMA ** (-neg_idx)
            a = jnp.concatenate([t_zero, t_pos, jnp.zeros((1, d), v.dtype), t_neg], axis=0)
            m = 2 * n
            y = jnp.fft.irfft(jnp.fft.rfft(a, n=m, axis=0)[None] * jnp.fft.rfft(v, n=m, axis=1), n=m, axis=1)
            return y[:, :n].astype(v.dtype)
        rpe_params = (rpe_pos_w, rpe_ln_w, rpe_ln_b, rpe_fc_w, rpe_out_ln_w, rpe_out_ln_b, rpe_out_w)
        uv = jax.nn.silu(x @ uv_w)
        u, v = jnp.split(uv, 2, axis=-1)
        out = u * _tno(v, rpe_params)
        return out @ o_w

    def _L0_ffn_ref(x, W1, b1, W2, b2, Wr, br, gamma, beta):
        import jax, jax.numpy as jnp
        import numpy as np
        B, S, D, F, E, TOP_K = (4, 256, 128, 512, 8, 2)
        LN_EPS = 1e-05
        b, s, d = x.shape
        e = Wr.shape[1]
        rw = jax.nn.softmax(x.mean(axis=1) @ Wr + br, axis=-1)
        x_flat = x.reshape(-1, d)
        rw_tok = jnp.repeat(rw, s, axis=0)
        tk_w, tk_i = jax.lax.top_k(rw_tok, TOP_K)
        tk_w = jax.nn.softmax(tk_w, axis=-1)
        h = jax.nn.gelu(jnp.einsum('nd,edf->enf', x_flat, W1) + b1[:, None, :], approximate=False)
        expert_out = jnp.einsum('enf,efd->end', h, W2) + b2[:, None, :]
        onehot = jax.nn.one_hot(tk_i, e, dtype=x.dtype)
        cw = jnp.einsum('nk,nke->ne', tk_w, onehot)
        out = jnp.einsum('ne,end->nd', cw, expert_out).reshape(b, s, d)
        y = out + x
        mu = y.mean(axis=-1, keepdims=True)
        var = y.var(axis=-1, keepdims=True)
        return (y - mu) / jnp.sqrt(var + LN_EPS) * gamma + beta
    x = L0_attn_x
    xn = _layernorm(x, axis=-1)
    s = _L0_attn_ref(xn, L0_attn_uv_w, L0_attn_o_w, L0_attn_rpe_pos_w, L0_attn_rpe_ln_w, L0_attn_rpe_ln_b, L0_attn_rpe_fc_w, L0_attn_rpe_out_ln_w, L0_attn_rpe_out_ln_b, L0_attn_rpe_out_w)
    g = _silu(_L0_ffn_ref(xn, L0_ffn_W1, L0_ffn_b1, L0_ffn_W2, L0_ffn_b2, L0_ffn_Wr, L0_ffn_br, L0_ffn_gamma, L0_ffn_beta))
    x = x + s * g
    return x

_drawn_inputs = setup_inputs


def setup_inputs(seed=0):
    import zlib

    import numpy as np

    out = dict(_drawn_inputs(seed))
    spreads = {'L0_attn_rpe_ln_w': (1.0, 0.6),
     'L0_attn_rpe_ln_b': (0.0, 0.8),
     'L0_attn_rpe_out_ln_w': (1.0, 0.6),
     'L0_attn_rpe_out_ln_b': (0.0, 0.8),
     'L0_ffn_b1': (0.0, 0.8),
     'L0_ffn_b2': (0.0, 2.0),
     'L0_ffn_br': (0.0, 0.8),
     'L0_ffn_gamma': (1.0, 0.6),
     'L0_ffn_beta': (0.0, 0.8)}
    factors = {'L0_attn_uv_w': 3.683,
     'L0_attn_o_w': 3.736,
     'L0_attn_rpe_pos_w': 7.011,
     'L0_attn_rpe_fc_w': 4.802,
     'L0_attn_rpe_out_w': 3.892,
     'L0_ffn_W1': 8.0,
     'L0_ffn_W2': 8.0,
     'L0_ffn_Wr': 8.0}
    for name, (base, spread) in spreads.items():
        noise = np.random.default_rng([zlib.crc32(name.encode()), seed]).standard_normal(out[name].shape)
        drawn = base * np.exp(spread * noise) if base else spread * noise
        out[name] = jnp.asarray(drawn.astype(out[name].dtype))
    for name, factor in factors.items():
        out[name] = (out[name] * factor).astype(out[name].dtype)
    return out
```

```python
from contextlib import ExitStack

import numpy as np

import concourse.bass as bass
from concourse import mybir

ALU = mybir.AluOpType
ACT = mybir.ActivationFunctionType
AX = mybir.AxisListType.X
F32 = mybir.dt.float32
F32R = mybir.dt.float32r
U32 = mybir.dt.uint32

P = 128
B, S, D = 8, 512, 128
E, F, TOPK = 8, 512, 2
R, L = 32, 3
NT = S // P
NC = S // 2 // P
KC = S // P
LC = S // P
FC = F // P
RG = P // R
PW = 2 * S // RG
GB = 4
HT = TOPK * FC
EPS = 1e-5
GAMMA = 0.99

LAYER_AT = [4, 6, 8, 10, 12]
STEPS = 13
ROUTER_AT = B + 1
LAYERS_BEFORE_ROUTER = sum(at < ROUTER_AT for at in LAYER_AT)
FORTH, BACK = (1, 3), (2, 4)
YT_AT = [16, 24, 32, 40, 44, 49, 56]
S_AT = [21, 28, 36, 43, 48, 54, 60]
TANH_AT = [22, 30, 38, 45, 50, 55, 62]
POOL_JOBS = [
    [],
    [("spectrum", 0), ("spectrum", 1), ("spectrum", 2), ("spectrum", 3)],
    [("fold", 4), ("fold", 5), ("gate", 0), ("fold", 6), ("fold", 7)],
    [("spectrum", 4), ("gate", 1), ("spectrum", 5), ("spectrum", 6), ("spectrum", 7)],
    [("gate", 2)],
    [("gate", 3), ("gate", 4)],
    [("gate", 5)],
    [("gate", 6), ("gate", 7)],
]
DVE_JOBS = [
    [("", 0)],
    [("products", 0), ("products", 1), ("products", 2), ("products", 3)],
    [("norm", 0), ("conv", 0), ("split", 4), ("conv", 1), ("split", 5), ("conv", 2), ("split", 6),
     ("result", 0), ("conv", 3), ("split", 7)],
    [("products", 4), ("norm", 1), ("products", 5), ("products", 6), ("result", 1), ("products", 7)],
    [("norm", 2), ("conv", 4), ("conv", 5), ("result", 2), ("conv", 6), ("conv", 7)],
    [("norm", 3), ("norm", 4), ("result", 3)],
    [("norm", 5), ("result", 4), ("result", 5)],
    [("norm", 6), ("result", 6), ("norm", 7), ("result", 7)],
]
STORES = [[], [], [0], [1], [2], [3], [4, 5], [6, 7]]
RELOADS = [[0, 1, 2, 3], [], [4], [5], [6], [7], [], []]


def shape_tables():
    k = (np.arange(S) + 0.5) * (2 * np.pi / (2 * S))
    n = S / 2 - 0.5 - np.arange(S // 2)
    cs = np.stack([np.cos(np.outer(n, k)), np.sin(np.outer(n, k))])
    fwd = cs.reshape(2, NC, P, S).transpose(2, 1, 0, 3)
    inv = cs.transpose(2, 0, 1).reshape(KC, P, 2, S // 2).transpose(1, 0, 2, 3)
    lag = np.arange(S)
    decay = GAMMA ** lag / S * np.where(lag == 0, 0.5, 1.0)
    al = np.stack([np.cos(np.outer(lag, k)), -np.sin(np.outer(lag, k))]) * decay[None, :, None]
    al = al.reshape(2, LC, P, S).transpose(2, 1, 0, 3)
    same = np.kron(np.eye(RG), np.ones((R, R)))
    sign = np.zeros((P, 4))
    for g, (even, odd) in enumerate([(0, 1), (2, 3), (0, 1), (2, 3)]):
        sign[g * R:(g + 1) * R, even] = 1
        sign[g * R:(g + 1) * R, odd] = 1 if g < 2 else -1
    c128 = np.concatenate([np.eye(P), same, sign], axis=1)
    rep = np.tile(np.eye(R), (1, RG))
    half = np.arange(PW)
    pos = np.stack([half, half + PW, -half, -half - PW])
    mask4 = np.kron(np.eye(RG), np.ones((1, R)))
    c4 = np.concatenate([pos, mask4], axis=1)
    c8 = np.concatenate([np.tile(np.arange(E), (B, 1)), np.eye(B), np.ones((B, P))], axis=1)
    f = np.float32
    c32 = np.zeros((R, P + PW + P))
    c32[:, 0:P] = rep
    c32[0:RG, P:] = c4
    wide = np.zeros((P, c128.shape[1] + c8.shape[1]))
    wide[:, 0:c128.shape[1]] = c128
    wide[0:B, c128.shape[1]:] = c8
    return {"fwd": fwd.reshape(P, -1).astype(f), "inv": inv.reshape(P, -1).astype(f),
            "lag": al.reshape(P, -1).astype(f), "c128": wide.astype(f), "c32": c32.astype(f)}


def build(nc, x, uv_w, o_w, pos_w, ln_w, ln_b, fc_w, out_ln_w, out_ln_b, out_w,
          W1, b1, W2, b2, Wr, br, gamma, beta, t_fwd, t_inv, t_lag, t_c128, t_c32, out):
    with ExitStack() as ctx:
        def sb(name, shape, dt=F32):
            return ctx.enter_context(nc.sbuf_tensor(name, shape, dt))

        def sem(name):
            return ctx.enter_context(nc.semaphore(name))

        NX = NR = 4
        x_ring = sb("x_ring", [P, NX, NT, D])
        xn = sb("xn", [P, 2, NT, D])
        xT_hi = sb("xT_hi", [P, B, S], F32R)
        xT_lo = sb("xT_lo", [P, B, S], F32R)
        uT = sb("uT", [P, B, S])
        vt = sb("vt", [P, GB, 2, NC, D])
        pm = sb("pm", [P, 2, 2, NC, D])
        pm_hi = sb("pm_hi", [P, 2, NC, GB, D], F32R)
        pm_lo = sb("pm_lo", [P, 2, NC, GB, D], F32R)
        Y = sb("Y", [P, KC, 2, GB, D])
        prod = sb("prod", [P, 4, GB, D])
        A_sb = sb("A_sb", [P, KC, 2, D])
        cs_hi = sb("cs_hi", [P, NC, 2, S], F32R)
        cs_lo = sb("cs_lo", [P, NC, 2, S], F32R)
        inv_sb = sb("inv_sb", [P, KC, 2, S // 2])
        w1_raw = sb("w1_raw", [P, TOPK, F])
        w1_hi = sb("w1_hi", [P, 2, TOPK, F], F32R)
        w1_lo = sb("w1_lo", [P, 2, TOPK, F], F32R)
        w2_s = sb("w2_s", [P, 2, TOPK, FC, D])
        NH = 4
        h_ring = sb("h_ring", [P, NH, S])
        O_sb = sb("O_sb", [P, 2, S // 2])
        conv = sb("conv", [P, S])
        NY = 3
        yT = sb("yT", [P, NY, S])
        yb = sb("yb", [P, 2, NT, D])
        zb = sb("zb", [P, 2, NT, D])
        th = sb("th", [P, 2, NT, D])
        uvw_hi = sb("uvw_hi", [P, 2 * D], F32R)
        uvw_lo = sb("uvw_lo", [P, 2 * D], F32R)
        ow_sb = sb("ow_sb", [P, D])
        gam = sb("gam", [P, D])
        bet = sb("bet", [P, D])
        c128 = sb("c128", [P, 2 * P + 4 + E + B + P])
        stats = sb("stats", [P, NT, 6])
        mv = sb("mv", [P, B, NT, 2])
        rstd = sb("rstd", [P, B, NT])
        ystats = sb("ystats", [P, NT, 6])
        ymv = sb("ymv", [P, NT, 2])
        yrstd = sb("yrstd", [P, NT])
        xsum = sb("xsum", [P, B])
        xmean = sb("xmean", [P, B])
        wr_sb = sb("wr_sb", [P, E])
        br_sb = sb("br_sb", [B, E])
        br8 = br_sb[:]
        logit = sb("logit", [B, E])
        cw_sb = sb("cw_sb", [B, TOPK])
        b2_sb = sb("b2_sb", [E, D])
        ex = sb("ex", [B, E])
        rw = sb("rw", [B, E])
        top8 = sb("top8", [B, 8])
        rx = sb("rx", [B, 8])
        idx = sb("idx", [B, 8], U32)
        idxf = sb("idxf", [B, 8])
        onehot = sb("onehot", [B, 3, E])
        diag = sb("diag", [B, TOPK, B])
        selT = sb("selT", [E, 3, B])
        b1_sel = sb("b1_sel", [P, FC, TOPK, B])
        b2_mix = sb("b2_mix", [P, B])
        cw_all = sb("cw_all", [P, TOPK, B])
        lnT = sb("lnT", [P, 8])
        same32 = sb("same32", [P, P])
        minus_half = sb("minus_half", [P, 8])
        root = sb("root", [P, 8])
        layer_var = sb("layer_var", [P, 8])
        layer_r = sb("layer_r", [P, 8])

        def flat(t):
            return t.rearrange("p a b -> p (a b)")

        lag_sb = Y[:].rearrange("p a r b d -> p (a r b d)").rearrange("p (l r k) -> p l r k", l=LC, r=2)
        teto = prod[:, 0:2]
        cs_raw = w2_s[:].rearrange("p a j c d -> p (a j c d)")
        uvw = O_sb[:].rearrange("p a i -> p (a i)")[:, 0:2 * D]
        b1_sb = conv[0:E, :]
        c32 = yT[:].rearrange("p a s -> p (a s)")[0:R, 0:P + PW + P]
        act, sq = flat(zb[:, 0])[:, 0:PW], flat(zb[:, 0])[:, PW:2 * PW]
        hc, nrm = flat(zb[:, 1])[:, 0:PW], flat(zb[:, 1])[:, PW:2 * PW]
        root_b = prod[:, 2].rearrange("p b d -> p (b d)")[:, 0:PW]
        fc_bd = th[:, 0, 0:L].rearrange("p l (g j) -> p l g j", g=RG)
        ow_v = th[:, 1]
        y0, y1 = flat(yb[:, 0]), flat(yb[:, 1])
        fcow, rep = y0[0:R, 0:L * R + D], c32[:, 0:P]
        rows8, l0 = y0[0:8, 384:384 + R], y0[0:RG, 416:416 + R]
        rows32, L0 = y1[0:8, 0:P], y1[0:RG, P:2 * P]
        fcc = y1[:, 256:256 + L * R].rearrange("p (l j) -> p l j", l=L)
        fmean, lmean, l0c = y1[:, 384:384 + L], y1[0:RG, 400:402], y1[0:RG, 416:416 + R]
        ident, same, sign = c128[:, 0:P], c128[:, P:2 * P], c128[:, 2 * P:2 * P + 4]
        pos, mask4 = c32[0:RG, P:P + PW], c32[0:RG, P + PW:]
        c8 = c128[0:B, 2 * P + 4:]
        nmax, esum, gap, e1, cw = rx[:, 1:2], rx[:, 2:3], rx[:, 4:5], rx[:, 5:6], cw_sb[:]
        xR_hi, xR_lo = (w1_x[:, 1].rearrange("p j (r n) -> p (j r) n", r=2) for w1_x in (w1_hi, w1_lo))
        iota8, ident8, ones8 = c8[:, 0:E], c8[:, E:E + B], c8[:, E + B:E + B + P]

        bank = [ctx.enter_context(nc.psum_tensor(f"bank{n}", [P, 512], F32)) for n in range(8)]
        T_PS = bank[0:2] + bank[6:8]
        H_PS = bank[0:2]
        U_PS = OUT_PS = bank[2]
        V_PS = EO_PS = bank[3]
        R_PS = S_PS = bank[4]
        Q_PS = YT_PS = bank[5]
        A_PS = V_RI = bank[6:8]

        x_in = [sem(f"x_in{n}") for n in range(NX)]
        consts_in = sem("consts_in")
        rpe_in = sem("rpe_in")
        uvw_in = sem("uvw_in")
        cs_in = sem("cs_in")
        lag_in = sem("lag_in")
        late_in, last_in = sem("late_in"), sem("last_in")
        w1_in, w2_in = sem("w1_in"), [sem("w2_in0"), sem("w2_in1")]
        out_done = [sem(f"out_done{n}") for n in range(NX)]
        dve_step, pool_step = sem("dve_step"), sem("pool_step")
        act_step = sem("act_step")
        stats_done = sem("stats_done")
        xn_done = sem("xn_done")
        xT_ps, xhi_done, xrev_done, xlo_done = (
            sem("xT_ps"), sem("xhi_done"), sem("xrev_done"), sem("xlo_done"))
        uvw_split = sem("uvw_split")
        u_ps, v_ps, u_done, v_done = sem("u_ps"), sem("v_ps"), sem("u_done"), sem("v_done")
        pm_done, pm_split = sem("pm_done"), sem("pm_split")
        rpe_pe, rpe_ready = sem("rpe_pe"), sem("rpe_ready")
        hc_ps, sq_done, var_ps, nrm_done, act_done = (
            sem("hc_ps"), sem("sq_done"), sem("var_ps"), sem("nrm_done"), sem("act_done"))
        hc_done, varT_done, layer_r_done, root_b_done, root_ps = (
            sem("hc_done"), sem("varT_done"), sem("layer_r_done"), sem("root_b_done"), sem("root_ps"))
        ystats_done, yrstd_done = sem("ystats_done"), sem("yrstd_done")
        teto_ps, teto_done, A_ps, A_done = sem("teto_ps"), sem("teto_done"), sem("A_ps"), sem("A_done")
        cs_hi_done, cs_split = sem("cs_hi_done"), sem("cs_split")
        xmean_done, logit_ps, nmax_done, exp_done, gap_done, exp2_done = (
            sem("xmean_done"), sem("logit_ps"), sem("nmax_done"), sem("exp_done"), sem("gap_done"),
            sem("exp2_done"))
        idx_done, pick_done, pickT_ps, pickT_done, sel_ps, sel_done = (
            sem("idx_done"), sem("pick_done"), sem("pickT_ps"), sem("pickT_done"), sem("sel_ps"),
            sem("sel_done"))
        w1_hi_done, w1_split, w2_scaled = sem("w1_hi_done"), sem("w1_split"), sem("w2_scaled")
        h_ps, h_done, w2_mm = sem("h_ps"), sem("h_done"), sem("w2_mm")
        yT_done, y_ps, y_read = sem("yT_done"), sem("y_ps"), sem("y_read")
        rstd_done = sem("rstd_done")
        xn2_done, z_done, zg_done, th_done = sem("xn2_done"), sem("z_done"), sem("zg_done"), sem("th_done")
        s_ps, s_read, res_done = sem("s_ps"), sem("s_read"), sem("res_done")
        vre_ps, vim_ps, vre_read, vim_read, Y_done = (
            sem("vre_ps"), sem("vim_ps"), sem("vre_read"), sem("vim_read"), sem("Y_done"))
        eo_ps, O_done, eo_read, conv_done = sem("eo_ps"), sem("O_done"), sem("eo_read"), sem("conv_done")

        x_v = x.rearrange("b (t p) d -> b p t d", p=P)
        out_v = out.rearrange("b (t p) d -> b p t d", p=P)
        w2_v = W2.rearrange("e (c p) d -> e p c d", p=P)
        block = ctx.enter_context(nc.Block())
        def bcast(ap, shape):
            return ap.broadcast_to(list(shape))

        @block.sync
        def _(sp):
            def load_x(n):
                if n >= NX and n < B:
                    sp.wait_ge(xn_done, n - NX + 1)
                sp.dma_start(x_ring[:, n % NX], x_v[n]).then_inc(x_in[n % NX], 16)

            def reload_x(b):
                if b >= NX:
                    sp.wait_ge(out_done[b % NX], 16)
                sp.dma_start(x_ring[:, b % NX], x_v[b]).then_inc(x_in[b % NX], 16)

            load_x(0)
            load_x(1)
            sp.dma_start(uvw, uv_w).then_inc(uvw_in, 16)
            for b in range(2, NX):
                load_x(b)
            for b in range(NX, B):
                load_x(b)
            for dst, src in ((wr_sb[:], Wr), (br8, br.partition_broadcast(B)),
                             (b1_sb, b1), (b2_sb[:], b2)):
                sp.dma_start(dst, src).then_inc(late_in, 16)
            sp.dma_start(cs_raw, t_fwd).then_inc(cs_in, 16)
            sp.dma_start(Y[:].rearrange("p a r b d -> p (a r b d)"), t_lag).then_inc(lag_in, 16)

            sp.wait_ge(idx_done, 1)
            chosen = {}

            def fetch_w1(b):
                if b >= 1:
                    sp.wait_ge(w1_split, TOPK * b)
                for j in range(TOPK):
                    chosen[b, j] = sp.value_load(idx[b:b + 1, j:j + 1], min_val=0, max_val=E - 1)
                    sp.dma_start(w1_raw[:, j, :], W1[bass.ds(chosen[b, j], 1), :, :]
                                 .rearrange("e d f -> d (e f)")).then_inc(w1_in, 16)

            def fetch_w2(b):
                if b == 0:
                    sp.wait_ge(cs_split, 1)
                if b >= 2:
                    sp.wait_ge(w2_mm, HT * (b - 1))
                for j in range(TOPK):
                    e = sp.value_load(idx[b:b + 1, j:j + 1], min_val=0, max_val=E - 1)
                    sp.dma_start(w2_s[:, b % 2, j], w2_v[bass.ds(e, 1), :, :, :]
                                 .rearrange("e p c d -> p (e c) d")).then_inc(w2_in[b % 2], 16)

            fetch_w1(0)
            fetch_w2(0)
            for dst, src in ((ow_sb[:], o_w), (gam[:], gamma.partition_broadcast(P)),
                             (bet[:], beta.partition_broadcast(P)),
                             (inv_sb[:].rearrange("p a r i -> p (a r i)"), t_inv)):
                sp.dma_start(dst, src).then_inc(last_in, 16)
            sp.wait_ge(xn_done, B)
            for b in range(B):
                if b + 1 < B:
                    fetch_w1(b + 1)
                    fetch_w2(b + 1)
                for n in STORES[b]:
                    sp.wait_ge(res_done, n + 1)
                    sp.dma_start(out_v[n], x_ring[:, n % NX]).then_inc(out_done[n % NX], 16)
                for n in RELOADS[b]:
                    reload_x(n)
            for n in range(NX):
                sp.wait_ge(out_done[n], 16 * (B // NX))

        @block.scalar
        def _(act_e):
            for dst, src in ((c128[:], t_c128),):
                act_e.dma_start(dst, src).then_inc(consts_in, 16)
            for dst, src in ((c32, t_c32), (l0, pos_w.rearrange("a r -> (a r)").partition_broadcast(RG)),
                             (rows8[0:L], ln_w), (rows8[L:2 * L], ln_b),
                             (rows8[2 * L:2 * L + 1], out_ln_w.unsqueeze(0)),
                             (rows8[2 * L + 1:2 * L + 2], out_ln_b.unsqueeze(0)),
                             (fcow[:, 0:L * R].rearrange("f (l j) -> f l j", l=L),
                              fc_w.rearrange("l f j -> f l j")),
                             (fcow[:, L * R:L * R + D], out_w)):
                act_e.dma_start(dst, src).then_inc(rpe_in, 16)

            def xn_hi(b):
                act_e.wait_ge(xT_ps, b + 1)
                nc.scalar.activation(xT_hi[:, b, :], T_PS[b % NR][:], ACT.Copy,
                                     accum_out=xsum[:, b:b + 1]).then_inc(xhi_done, 1)
                if b >= NR:
                    act_e.wait_ge(v_ps, b - NR + 1)
                nc.scalar.activation(xR_hi[:, b % NR], T_PS[b % NR][:, S - 1:S // 2 - 1:-1],
                                     ACT.Copy).then_inc(xrev_done, 1)

            def layer_square(n):
                act_e.wait_ge(hc_ps, n + 1)
                nc.scalar.activation(sq, R_PS[:, 0:PW], ACT.Square).then_inc(sq_done, 1)
                nc.scalar.activation(hc, R_PS[:, 0:PW], ACT.Copy).then_inc(hc_done, 1)

            def layer_silu(n):
                scale, bias = (n, L + n) if n < L else (2 * L, 2 * L + 1)
                act_e.wait_ge(nrm_done, n + 1)
                nc.scalar.activation(act, nrm, ACT.Silu, bias=lnT[:, bias:bias + 1],
                                     scale=lnT[:, scale:scale + 1]).then_inc(act_done, 1)

            def router_exponentials():
                act_e.wait_ge(nmax_done, 1)
                nc.scalar.activation(ex[:], logit[:], ACT.Exp, bias=nmax,
                                     accum_out=esum).then_inc(exp_done, 1)
                act_e.wait_ge(gap_done, 1)
                nc.scalar.activation(e1, gap, ACT.Exp).then_inc(exp2_done, 1)

            def silu_uv(b):
                act_e.wait_ge(u_ps, b + 1)
                nc.scalar.activation(uT[:, b, :], U_PS[:], ACT.Silu).then_inc(u_done, 1)
                act_e.wait_ge(v_ps, b + 1)
                if b >= GB:
                    act_e.wait_ge(pm_done, b - GB + 1)
                nc.scalar.activation(vt[:, b % GB].rearrange("p r c d -> p (r c d)"), V_PS[:],
                                     ACT.Silu).then_inc(v_done, 1)

            for b in range(STEPS):
                if b in LAYER_AT and LAYER_AT.index(b) < L + 2 and LAYER_AT.index(b) >= 1:
                    layer_silu(LAYER_AT.index(b) - 1)
                if 1 <= b <= B:
                    xn_hi(b - 1)
                if b in LAYER_AT and LAYER_AT.index(b) < L + 1:
                    layer_square(LAYER_AT.index(b))
                if 3 <= b < B + 3:
                    silu_uv(b - 3)
                if b == B:
                    act_e.wait_ge(cs_in, 16)
                    nc.scalar.activation(cs_hi[:].rearrange("p c r k -> p (c r k)"), cs_raw,
                                         ACT.Copy).then_inc(cs_hi_done, 1)
                if b == ROUTER_AT:
                    router_exponentials()
            act_e.wait_ge(teto_ps, 1)
            for n in range(2):
                nc.scalar.activation(teto[:, n].rearrange("p q d -> p (q d)"),
                                     A_PS[n][:], ACT.Copy).then_inc(teto_done, 1)

            def w1_upper(b):
                act_e.wait_ge(w1_in, 16 * TOPK * (b + 1))
                if b == 1:
                    act_e.wait_ge(v_ps, B)
                if b >= 2:
                    act_e.wait_ge(h_ps, HT * (b - 1))
                for j in range(TOPK):
                    nc.scalar.activation(w1_hi[:, b % 2, j], w1_raw[:, j], ACT.Copy).then_inc(w1_hi_done, 1)

            def gelu(n):
                b, j, c = n // HT, n % HT // FC, n % FC
                act_e.wait_ge(h_ps, n + 1)
                if n >= NH:
                    act_e.wait_ge(w2_mm, n - NH + 1)
                nc.scalar.activation(h_ring[:, n % NH], H_PS[n % 2][:], ACT.Gelu,
                                     bias=b1_sel[:, c, j, b:b + 1]).then_inc(h_done, 1)

            def experts_out(b):
                act_e.wait_ge(w2_mm, HT * (b + 1))
                if b >= NY:
                    act_e.wait_ge(y_ps, b - NY + 1)
                nc.scalar.activation(yT[:, b % NY], OUT_PS[:], ACT.Identity,
                                     bias=b2_mix[:, b:b + 1]).then_inc(yT_done, 1)

            def odd_part(b):
                act_e.wait_ge(eo_ps, b + 1)
                if b >= 2:
                    act_e.wait_ge(eo_read, b - 1)
                nc.scalar.activation(O_sb[:, b % 2], EO_PS[:, S // 2:S], ACT.Copy).then_inc(O_done, 1)

            def gate_tanh(b):
                act_e.wait_ge(zg_done, b + 1)
                if b >= 2:
                    act_e.wait_ge(res_done, b - 1)
                nc.scalar.activation(th[:, b % 2], zb[:, b % 2], ACT.Tanh, scale=0.5).then_inc(th_done, 1)

            w1_upper(0)
            act_e.wait_ge(sel_done, 1)
            for b in range(B):
                if b >= 1:
                    experts_out(b - 1)
                for i in range(HT):
                    n = HT * b + i
                    gelu(n)
                    if i == 0 and b + 1 < B:
                        w1_upper(b + 1)
                    if b == 0 and i == HT - 1:
                        act_e.wait_ge(A_ps, 1)
                        for m in range(2):
                            nc.scalar.activation(
                                A_sb[:, 2 * m:2 * m + 2].rearrange("p a r d -> p (a r d)"),
                                A_PS[m][:], ACT.Copy).then_inc(A_done, 1)
                    if b in BACK and i in (2, 4, 6, 7):
                        odd_part(GB * BACK.index(b) + (i - 1) // 2)
                    if n in TANH_AT:
                        gate_tanh(TANH_AT.index(n))
            experts_out(B - 1)
            gate_tanh(B - 1)

        @block.gpsimd
        def _(pool):
            steps = [0]

            def step(ins):
                steps[0] += 1
                ins.then_inc(pool_step, 1)
                pool.wait_ge(pool_step, steps[0])

            def inverse_root(out_r, var, n):
                step(nc.gpsimd.tensor_scalar(root[:, 0:n], var, EPS, None, ALU.add))
                return nc.gpsimd.tensor_tensor(out_r, root[:, 0:n], minus_half[:, 0:n], ALU.pow)

            def gate_root(b):
                pool.wait_ge(ystats_done, b + 1)
                pool.wait_ge(*((rstd_done, B) if b == 0 else (yrstd_done, b)))
                inverse_root(yrstd[:], ymv[:, :, 1], NT).then_inc(yrstd_done, 1)

            def layer_root(n):
                pool.wait_ge(varT_done, n + 1)
                if n >= 1:
                    pool.wait_ge(layer_r_done, n)
                nc.gpsimd.tensor_tensor(layer_r[:], layer_var[:], minus_half[:], ALU.pow).then_inc(
                    layer_r_done, 1)

            def rows_root(b):
                pool.wait_ge(stats_done, b + 1)
                if b >= 1:
                    pool.wait_ge(rstd_done, b)
                inverse_root(rstd[:, b], mv[:, b, :, 1], NT).then_inc(rstd_done, 1)

            def fold(b):
                pool.wait_ge(v_done, b + 1)
                if b >= 2:
                    pool.wait_ge(pm_split, b - 1)
                nc.gpsimd.tensor_tensor(pm[:, b % 2, 0], vt[:, b % GB, 0], vt[:, b % GB, 1], ALU.add)
                nc.gpsimd.tensor_tensor(pm[:, b % 2, 1], vt[:, b % GB, 0], vt[:, b % GB, 1],
                                        ALU.subtract).then_inc(pm_done, 1)

            def spectrum(q):
                pool.wait_ge(vim_read, q + 1)
                if q == KC:
                    pool.wait_ge(eo_ps, GB)
                nc.gpsimd.tensor_tensor(Y[:, q % KC, 0], prod[:, 0], prod[:, 2], ALU.subtract)
                nc.gpsimd.tensor_tensor(Y[:, q % KC, 1], prod[:, 1], prod[:, 3],
                                        ALU.add).then_inc(Y_done, 1)

            def w1_lower(b):
                for j in range(TOPK):
                    pool.wait_ge(w1_hi_done, TOPK * b + j + 1)
                    nc.gpsimd.tensor_tensor(w1_lo[:, b % 2, j], w1_raw[:, j], w1_hi[:, b % 2, j],
                                            ALU.subtract).then_inc(w1_split, 1)

            def gate_affine(b):
                pool.wait_ge(z_done, b + 1)
                step(nc.gpsimd.tensor_tensor(zb[:, b % 2], zb[:, b % 2],
                                             bcast(gam[:].unsqueeze(1), [P, NT, D]), ALU.mult))
                nc.gpsimd.tensor_tensor(zb[:, b % 2], zb[:, b % 2],
                                        bcast(bet[:].unsqueeze(1), [P, NT, D]),
                                        ALU.add).then_inc(zg_done, 1)

            step(nc.gpsimd.memset(minus_half[:], -0.5))
            for b in range(STEPS):
                if b < B:
                    rows_root(b)
                if b - 1 in LAYER_AT and LAYER_AT.index(b - 1) < L + 1:
                    layer_root(LAYER_AT.index(b - 1))
                if 4 <= b < GB + 4:
                    fold(b - 4)
                if b == B:
                    pool.wait_ge(cs_hi_done, 1)
                    nc.gpsimd.tensor_tensor(cs_lo[:].rearrange("p c r k -> p (c r k)"), cs_raw,
                                            cs_hi[:].rearrange("p c r k -> p (c r k)"),
                                            ALU.subtract).then_inc(cs_split, 1)
            w1_lower(0)
            for b in range(B):
                if b + 1 < B:
                    w1_lower(b + 1)
                for what, n in POOL_JOBS[b]:
                    if what == "spectrum":
                        spectrum(n)
                    elif what == "fold":
                        fold(n)
                    else:
                        if n == 0:
                            pool.wait_ge(last_in, 16 * 4)
                        gate_root(n)
                        gate_affine(n)

        @block.vector
        def _(dve):
            steps = [0]

            def step(ins):
                steps[0] += 1
                ins.then_inc(dve_step, 1)
                dve.wait_ge(dve_step, steps[0])

            def row_stats(src, st, out_mv):
                for t in range(NT):
                    last = nc.vector.bn_stats(st[:, t], src[:, t])
                step(last)
                for t in range(NT):
                    last = nc.vector.bn_aggr(out_mv[:, t], st[:, t])
                return last

            def x_stats(b):
                dve.wait_ge(x_in[b % NX], 16 * (b // NX + 1))
                if b >= 1:
                    dve.wait_ge(stats_done, b)
                row_stats(x_ring[:, b % NX], stats, mv[:, b]).then_inc(stats_done, 1)

            def normalize(b):
                dve.wait_ge(rstd_done, b + 1)
                if b >= 2:
                    dve.wait_ge(xT_ps, b - 1)
                for t in range(NT):
                    last = nc.vector.tensor_scalar(xn[:, b % 2, t], x_ring[:, b % NX, t],
                                                   mv[:, b, t, 0:1], rstd[:, b, t:t + 1],
                                                   ALU.subtract, ALU.mult)
                last.then_inc(xn_done, 1)

            def normalize_again(b):
                dve.wait_ge(x_in[b % NX], 16 * (B // NX + b // NX + 1))
                for t in range(NT):
                    last = nc.vector.tensor_scalar(yb[:, b % 2, t], x_ring[:, b % NX, t],
                                                   mv[:, b, t, 0:1], rstd[:, b, t:t + 1],
                                                   ALU.subtract, ALU.mult)
                last.then_inc(xn2_done, 1)

            def w2_scale(b):
                dve.wait_ge(w2_in[b % 2], 16 * TOPK * (b // 2 + 1))
                for j in range(TOPK):
                    last = nc.vector.tensor_scalar(w2_s[:, b % 2, j], w2_s[:, b % 2, j],
                                                   cw_all[:, j, b:b + 1], None, ALU.mult)
                last.then_inc(w2_scaled, 1)

            def xn_lo(b):
                dve.wait_ge(xrev_done, b + 1)
                nc.vector.tensor_tensor(xT_lo[:, b, :], T_PS[b % NR][:], xT_hi[:, b, :],
                                        ALU.subtract)
                if b >= NR:
                    dve.wait_ge(v_ps, b - NR + 1)
                nc.vector.tensor_tensor(xR_lo[:, b % NR], T_PS[b % NR][:, S - 1:S // 2 - 1:-1],
                                        xR_hi[:, b % NR], ALU.subtract).then_inc(xlo_done, 1)

            def split_fold(b):
                dve.wait_ge(pm_done, b + 1)
                if b == GB:
                    dve.wait_ge(vim_ps, KC)
                step(nc.vector.tensor_copy(pm_hi[:, :, :, b % GB, :], pm[:, b % 2]))
                nc.vector.tensor_tensor(pm_lo[:, :, :, b % GB, :], pm[:, b % 2],
                                        pm_hi[:, :, :, b % GB, :], ALU.subtract).then_inc(pm_split, 1)

            def layer_eps(n):
                dve.wait_ge(var_ps, n + 1)
                nc.vector.tensor_scalar(layer_var[:], Q_PS[:, 0:8], EPS, None, ALU.add).then_inc(varT_done, 1)

            def layer_spread(n):
                dve.wait_ge(layer_r_done, n + 1)
                nc.vector.tensor_copy(root_b.rearrange("p (q j) -> p q j", j=R),
                                      bcast(layer_r[:].unsqueeze(2), [P, 8, R])).then_inc(root_b_done, 1)

            def layer_norm(n):
                dve.wait_ge(root_ps, n + 1)
                dve.wait_ge(hc_done, n + 1)
                nc.vector.tensor_tensor(nrm, Q_PS[:, PW:2 * PW], hc, ALU.mult).then_inc(nrm_done, 1)

            def position_weights():
                dve.wait_ge(rpe_in, 16 * 8)
                dve.wait_ge(consts_in, 16)
                nc.vector.tensor_copy(rows32.rearrange("r (g j) -> r g j", g=RG),
                                      bcast(rows8.unsqueeze(1), [8, RG, R]))
                step(nc.vector.tensor_reduce(lmean[:, 0:1], l0, AX, ALU.add))
                step(nc.vector.tensor_scalar(lmean[:, 1:2], lmean[:, 0:1], -1.0 / R, None, ALU.mult))
                step(nc.vector.tensor_scalar(l0c, l0, lmean[:, 1:2], None, ALU.add))
                nc.vector.tensor_tensor(L0.rearrange("r (g j) -> r g j", g=RG),
                                        bcast(l0c.unsqueeze(1), [RG, RG, R]),
                                        mask4.rearrange("r (g j) -> r g j", g=RG), ALU.mult)
                nc.vector.tensor_scalar(same32[:], same, 1.0 / R, None, ALU.mult).then_inc(rpe_ready, 1)

            def position_matrices():
                dve.wait_ge(rpe_pe, 1)
                nc.vector.tensor_copy(lnT[:], R_PS[:, 0:8])
                fc_ps = R_PS[:, P:P + L * R].rearrange("p (l j) -> p l j", l=L)
                step(nc.vector.tensor_reduce(fmean, fc_ps, AX, ALU.add))
                step(nc.vector.tensor_scalar(fmean, fmean, -1.0 / R, None, ALU.mult))
                step(nc.vector.tensor_tensor(fcc, fc_ps, bcast(fmean.unsqueeze(2), [P, L, R]), ALU.add))
                for n in range(L):
                    nc.vector.tensor_tensor(fc_bd[:, n], bcast(fcc[:, n].unsqueeze(1), [P, RG, R]),
                                            same.rearrange("p (g j) -> p g j", g=RG), ALU.mult)
                nc.vector.tensor_tensor(ow_v, bcast(R_PS[:, P + L * R:P + L * R + D].unsqueeze(1), [P, 4, D]),
                                        bcast(sign.unsqueeze(2), [P, 4, D]), ALU.mult).then_inc(rpe_ready, 1)

            def router_mean():
                dve.wait_ge(xhi_done, B)
                nc.vector.tensor_scalar(xmean[:], xsum[:], 1.0 / S, None, ALU.mult).then_inc(xmean_done, 1)

            def router_logits():
                dve.wait_ge(logit_ps, 1)
                step(nc.vector.tensor_tensor(logit[:], R_PS[0:B, 0:E], br8, ALU.add))
                step(nc.vector.tensor_reduce(rx[:, 0:1], logit[:], AX, ALU.max))
                nc.vector.tensor_scalar(nmax, rx[:, 0:1], -1.0, None, ALU.mult).then_inc(nmax_done, 1)

            def router_top():
                dve.wait_ge(exp_done, 1)
                step(nc.vector.reciprocal(rx[:, 3:4], esum))
                step(nc.vector.tensor_scalar(rw[:], ex[:], rx[:, 3:4], None, ALU.mult))
                step(nc.vector.max(top8[:], rw[:]))
                nc.vector.tensor_tensor(gap, top8[:, 1:2], top8[:, 0:1], ALU.subtract).then_inc(gap_done, 1)
                nc.vector.max_index(idx[:], top8[:], rw[:]).then_inc(idx_done, 1)
                dve.wait_ge(idx_done, 1)
                step(nc.vector.tensor_copy(idxf[:], idx[:]))
                for j in range(TOPK):
                    nc.vector.tensor_scalar(onehot[:, j], iota8, idxf[:, j:j + 1], None, ALU.is_equal)

            def router_mix():
                dve.wait_ge(exp2_done, 1)
                step(nc.vector.tensor_scalar(rx[:, 6:7], e1, 1.0, None, ALU.add))
                step(nc.vector.reciprocal(cw[:, 0:1], rx[:, 6:7]))
                step(nc.vector.tensor_tensor(cw[:, 1:2], e1, cw[:, 0:1], ALU.mult))
                for j in range(TOPK):
                    nc.vector.tensor_scalar(diag[:, j], ident8, cw[:, j:j + 1], None, ALU.mult)
                step(nc.vector.tensor_scalar(ex[:], onehot[:, 0], cw[:, 0:1], None, ALU.mult))
                nc.vector.scalar_tensor_tensor(out=onehot[:, 2], in0=onehot[:, 1], scalar=cw[:, 1:2],
                                               in1=ex[:], op0=ALU.mult, op1=ALU.add).then_inc(pick_done, 1)

            def router_picks():
                dve.wait_ge(pickT_ps, 1)
                nc.vector.tensor_copy(selT[:].rearrange("e q b -> e (q b)"),
                                      R_PS[0:E, 64:64 + 3 * B]).then_inc(pickT_done, 1)
                dve.wait_ge(sel_ps, 1)
                n1 = FC * TOPK * B
                o = 64 + n1
                nc.vector.tensor_copy(b1_sel[:].rearrange("p c j b -> p (c j b)"), Q_PS[:, 64:64 + n1])
                nc.vector.tensor_copy(b2_mix[:], Q_PS[:, o:o + B])
                nc.vector.tensor_copy(cw_all[:].rearrange("p j b -> p (j b)"),
                                      Q_PS[:, o + B:o + 3 * B]).then_inc(sel_done, 1)


            for b in range(STEPS):
                if b < B:
                    x_stats(b)
                if b == 1:
                    dve.wait_ge(uvw_in, 16)
                    step(nc.vector.tensor_copy(uvw_hi[:], uvw))
                    nc.vector.tensor_tensor(uvw_lo[:], uvw, uvw_hi[:], ALU.subtract).then_inc(uvw_split, 1)
                if b == LAYER_AT[0] - 1:
                    position_weights()
                if b == LAYER_AT[0]:
                    position_matrices()
                if b in LAYER_AT and LAYER_AT.index(b) >= 1:
                    layer_norm(LAYER_AT.index(b) - 1)
                if b == B + 1:
                    router_mean()
                if 1 <= b <= B:
                    normalize(b - 1)
                if b - 1 in LAYER_AT and LAYER_AT.index(b - 1) < L + 1:
                    layer_eps(LAYER_AT.index(b - 1))
                if 2 <= b < B + 2:
                    xn_lo(b - 2)
                if b == ROUTER_AT:
                    router_logits()
                if b - 1 in LAYER_AT and LAYER_AT.index(b - 1) < L + 1:
                    layer_spread(LAYER_AT.index(b - 1))
                if 5 <= b < GB + 5:
                    split_fold(b - 5)
                if b == ROUTER_AT:
                    router_top()
                if b == ROUTER_AT + 1:
                    router_mix()
                    router_picks()

            def products(q):
                kc = q % KC
                a_re = bcast(A_sb[:, kc, 0].unsqueeze(1), [P, GB, D])
                a_im = bcast(A_sb[:, kc, 1].unsqueeze(1), [P, GB, D])
                v_re = V_RI[0][:].rearrange("p (b d) -> p b d", b=GB)
                v_im = V_RI[1][:].rearrange("p (b d) -> p b d", b=GB)
                if q == 0:
                    dve.wait_ge(A_done, 2)
                if q >= 1:
                    dve.wait_ge(Y_done, q)
                dve.wait_ge(vre_ps, q + 1)
                nc.vector.tensor_tensor(prod[:, 0], v_re, a_re, ALU.mult)
                nc.vector.tensor_tensor(prod[:, 1], v_re, a_im, ALU.mult).then_inc(vre_read, 1)
                dve.wait_ge(vim_ps, q + 1)
                nc.vector.tensor_tensor(prod[:, 2], v_im, a_im, ALU.mult)
                nc.vector.tensor_tensor(prod[:, 3], v_im, a_re, ALU.mult).then_inc(vim_read, 1)

            def convolved(b):
                dve.wait_ge(O_done, b + 1)
                if b >= 1:
                    dve.wait_ge(conv_done, b)
                nc.vector.tensor_tensor(conv[:, 0:S // 2], EO_PS[:, 0:S // 2], O_sb[:, b % 2], ALU.add)
                nc.vector.tensor_tensor(conv[:, S - 1:S // 2 - 1:-1], EO_PS[:, 0:S // 2], O_sb[:, b % 2],
                                        ALU.subtract).then_inc(eo_read, 1)
                dve.wait_ge(eo_read, b + 1)
                nc.vector.tensor_tensor(uT[:, b, :], uT[:, b, :], conv[:], ALU.mult).then_inc(conv_done, 1)

            def gate_norm(b):
                dve.wait_ge(y_ps, b + 1)
                dve.wait_ge(xn2_done, b + 1)
                nc.vector.tensor_tensor(yb[:, b % 2].rearrange("p t d -> p (t d)"), YT_PS[:],
                                        yb[:, b % 2].rearrange("p t d -> p (t d)"),
                                        ALU.add).then_inc(y_read, 1)
                dve.wait_ge(y_read, b + 1)
                if b >= 1:
                    dve.wait_ge(z_done, b)
                row_stats(yb[:, b % 2], ystats, ymv).then_inc(ystats_done, 1)
                dve.wait_ge(yrstd_done, b + 1)
                for t in range(NT):
                    last = nc.vector.tensor_scalar(zb[:, b % 2, t], yb[:, b % 2, t], ymv[:, t, 0:1],
                                                   yrstd[:, t:t + 1], ALU.subtract, ALU.mult)
                last.then_inc(z_done, 1)

            def result(b):
                w = th[:, b % 2]
                dve.wait_ge(th_done, b + 1)
                step(nc.vector.scalar_tensor_tensor(out=w, in0=w, scalar=1.0, in1=zb[:, b % 2],
                                                    op0=ALU.add, op1=ALU.mult))
                dve.wait_ge(s_ps, b + 1)
                nc.vector.tensor_tensor(w, S_PS[:].rearrange("p (t d) -> p t d", t=NT), w,
                                        ALU.mult).then_inc(s_read, 1)
                dve.wait_ge(s_read, b + 1)
                nc.vector.scalar_tensor_tensor(out=x_ring[:, b % NX], in0=w, scalar=0.5,
                                               in1=x_ring[:, b % NX], op0=ALU.mult,
                                               op1=ALU.add).then_inc(res_done, 1)

            w2_scale(0)
            for b in range(B):
                for n, (what, m) in enumerate(DVE_JOBS[b]):
                    if n == min(1, len(DVE_JOBS[b]) - 1) and b + 1 < B:
                        w2_scale(b + 1)
                    if what == "products":
                        products(m)
                    elif what == "conv":
                        convolved(m)
                    elif what == "split":
                        split_fold(m)
                    elif what == "norm":
                        normalize_again(m)
                        gate_norm(m)
                    elif what == "result":
                        result(m)

        @block.tensor
        def _(pe):
            def three(out_ps, w_hi, w_lo, m_hi, m_lo, start=True, stop=True):
                nc.tensor.matmul(out_ps, w_hi, m_hi, start=start, stop=False)
                nc.tensor.matmul(out_ps, w_hi, m_lo, start=False, stop=False)
                return nc.tensor.matmul(out_ps, w_lo, m_hi, start=False, stop=stop)

            def transpose_x(b):
                pe.wait_ge(xn_done, b + 1)
                if b == 0:
                    pe.wait_ge(consts_in, 16)
                if b >= NR:
                    pe.wait_ge(xlo_done, b - NR + 1)
                for t in range(NT):
                    last = nc.tensor.transpose(T_PS[b % NR][:, t * P:(t + 1) * P], xn[:, b % 2, t], ident)
                last.then_inc(xT_ps, 1)

            def project(b):
                pe.wait_ge(xlo_done, b + 1)
                if b == 0:
                    pe.wait_ge(uvw_split, 1)
                if b >= 1:
                    pe.wait_ge(u_done, b)
                three(U_PS[:], uvw_hi[:, 0:D], uvw_lo[:, 0:D], xT_hi[:, b], xT_lo[:, b]).then_inc(u_ps, 1)
                if b >= 1:
                    pe.wait_ge(v_done, b)
                for r in range(2):
                    for c in range(NC):
                        rows = slice(c * P, (c + 1) * P)
                        hi, lo = (xT_hi[:, b, rows], xT_lo[:, b, rows]) if r == 0 else \
                            (xR_hi[:, b % NR, rows], xR_lo[:, b % NR, rows])
                        o = (r * NC + c) * D
                        last = three(V_PS[:, o:o + D], hi, lo,
                                     uvw_hi[:, D:2 * D], uvw_lo[:, D:2 * D])
                last.then_inc(v_ps, 1)

            def layer_product(n):
                if n == 0:
                    pe.wait_ge(rpe_ready, 2)
                    nc.tensor.matmul(R_PS[:, 0:PW], L0, pos, start=True, stop=True).then_inc(hc_ps, 1)
                else:
                    pe.wait_ge(act_done, n)
                    if n == LAYERS_BEFORE_ROUTER:
                        pe.wait_ge(nmax_done, 1)
                    nc.tensor.matmul(R_PS[:, 0:PW], fc_bd[:, n - 1].rearrange("p g j -> p (g j)"), act,
                                     start=True, stop=True).then_inc(hc_ps, 1)

            def layer_variance(n):
                pe.wait_ge(sq_done, n + 1)
                for cc in range(2):
                    last = nc.tensor.matmul(Q_PS[:, cc * RG:(cc + 1) * RG], sq[:, cc * P:(cc + 1) * P],
                                            same32[:, 0:P:R], start=True, stop=True)
                last.then_inc(var_ps, 1)

            def layer_root_back(n):
                pe.wait_ge(root_b_done, n + 1)
                for cc in range(2):
                    last = nc.tensor.transpose(Q_PS[:, PW + cc * P:PW + (cc + 1) * P],
                                               root_b[:, cc * P:(cc + 1) * P], ident)
                last.then_inc(root_ps, 1)

            def even_odd_lags():
                pe.wait_ge(act_done, L + 1)
                for cc in range(2):
                    last = nc.tensor.matmul(A_PS[cc][:], act[:, cc * P:(cc + 1) * P],
                                            ow_v.rearrange("p q d -> p (q d)"), start=True, stop=True)
                last.then_inc(teto_ps, 1)

            def filter_spectrum(kc):
                if kc == 0:
                    pe.wait_ge(teto_done, 2)
                    pe.wait_ge(lag_in, 16)
                if True:
                    for ri in range(2):
                        o = (kc % 2) * 2 * D + ri * D
                        for lc in range(LC):
                            last = nc.tensor.matmul(A_PS[kc // 2][:, o:o + D],
                                                    lag_sb[:, lc, ri, kc * P:(kc + 1) * P],
                                                    teto[:, lc % 2, 2 * (lc // 2) + ri],
                                                    start=(lc == 0), stop=(lc == LC - 1))
                if kc == KC - 1:
                    last.then_inc(A_ps, 1)

            def router_logits():
                pe.wait_ge(xmean_done, 1)
                pe.wait_ge(late_in, 16 * 4)
                pe.wait_ge(hc_done, LAYERS_BEFORE_ROUTER)
                nc.tensor.matmul(R_PS[0:B, 0:E], xmean[:], wr_sb[:], start=True, stop=True).then_inc(logit_ps, 1)

            def router_picks():
                pe.wait_ge(pick_done, 1)
                pe.wait_ge(hc_done, LAYERS_BEFORE_ROUTER + 1)
                for q in range(3):
                    last = nc.tensor.transpose(R_PS[0:E, 64 + q * B:64 + (q + 1) * B], onehot[:, q], ident8)
                last.then_inc(pickT_ps, 1)
                pe.wait_ge(pickT_done, 1)
                picks = selT[:, 0:TOPK].rearrange("e j b -> e (j b)")
                w = TOPK * B
                for c in range(FC):
                    nc.tensor.matmul(Q_PS[:, 64 + c * w:64 + (c + 1) * w], b1_sb[:, c * P:(c + 1) * P], picks,
                                     start=True, stop=True)
                o = 64 + FC * w
                nc.tensor.matmul(Q_PS[:, o:o + B], b2_sb[:], selT[:, 2], start=True, stop=True)
                nc.tensor.matmul(Q_PS[:, o + B:o + B + w], ones8, diag[:].rearrange("b j c -> b (j c)"),
                                 start=True, stop=True).then_inc(sel_ps, 1)


            for b in range(STEPS):
                if b in LAYER_AT and LAYER_AT.index(b) < L + 1:
                    layer_product(LAYER_AT.index(b))
                if b == B + 1:
                    router_logits()
                if 1 <= b <= B:
                    transpose_x(b - 1)
                if b == LAYER_AT[0] - 1:
                    pe.wait_ge(rpe_ready, 1)
                    nc.tensor.transpose(R_PS[:, 0:8], rows32, ident[0:8, 0:8])
                    nc.tensor.matmul(R_PS[:, P:P + L * R + D], rep, fcow, start=True,
                                     stop=True).then_inc(rpe_pe, 1)
                if b in LAYER_AT and LAYER_AT.index(b) < L + 1:
                    layer_variance(LAYER_AT.index(b))
                if 3 <= b < B + 3:
                    project(b - 3)
                if b == B + 2:
                    router_picks()
                if b - 1 in LAYER_AT and LAYER_AT.index(b - 1) < L + 1:
                    layer_root_back(LAYER_AT.index(b - 1))
            even_odd_lags()

            def hidden(n):
                b, j, c = n // HT, n % HT // FC, n % FC
                if n % FC == 0:
                    pe.wait_ge(w1_split, n // FC + 1)
                if n >= 2:
                    pe.wait_ge(h_done, n - 1)
                col = slice(c * P, (c + 1) * P)
                three(H_PS[n % 2][:], w1_hi[:, b % 2, j, col], w1_lo[:, b % 2, j, col],
                      xT_hi[:, b], xT_lo[:, b]).then_inc(h_ps, 1)

            def expert_out(n):
                b, i = n // HT, n % HT
                if i == 0:
                    pe.wait_ge(w2_scaled, b + 1)
                    if b >= 1:
                        pe.wait_ge(yT_done, b)
                pe.wait_ge(h_done, n + 1)
                nc.tensor.matmul(OUT_PS[:], w2_s[:, b % 2, i // FC, i % FC], h_ring[:, n % NH],
                                 start=(i == 0), stop=(i == HT - 1)).then_inc(w2_mm, 1)

            def transform(q):
                kc = q % KC
                if q == 0:
                    pe.wait_ge(cs_split, 1)
                    pe.wait_ge(A_done, 2)
                if kc == 0:
                    pe.wait_ge(pm_split, GB * (q // KC + 1))
                for ri, (done, read) in enumerate(((vre_ps, vre_read), (vim_ps, vim_read))):
                    if q >= 1:
                        pe.wait_ge(read, q)
                    for c in range(NC):
                        col = slice(kc * P, (kc + 1) * P)
                        last = three(V_RI[ri][:], cs_hi[:, c, ri, col], cs_lo[:, c, ri, col],
                                     pm_hi[:, ri, c].rearrange("p b d -> p (b d)"),
                                     pm_lo[:, ri, c].rearrange("p b d -> p (b d)"),
                                     start=(c == 0), stop=(c == NC - 1))
                    last.then_inc(done, 1)

            def transform_back(b):
                pe.wait_ge(Y_done, KC * (b // GB + 1))
                if b == 0:
                    pe.wait_ge(last_in, 16 * 4)
                if b >= 1:
                    pe.wait_ge(eo_read, b)
                for ri in range(2):
                    for kc in range(KC):
                        last = nc.tensor.matmul(EO_PS[:, ri * S // 2:(ri + 1) * S // 2],
                                                Y[:, kc, ri, b % GB], inv_sb[:, kc, ri],
                                                start=(kc == 0), stop=(kc == KC - 1))
                last.then_inc(eo_ps, 1)

            def transpose_y(b):
                pe.wait_ge(yT_done, b + 1)
                if b >= 1:
                    pe.wait_ge(y_read, b)
                for t in range(NT):
                    last = nc.tensor.transpose(YT_PS[:, t * P:(t + 1) * P],
                                               yT[:, b % NY, t * P:(t + 1) * P], ident)
                last.then_inc(y_ps, 1)

            def mixed(b):
                pe.wait_ge(conv_done, b + 1)
                if b == 0:
                    pe.wait_ge(last_in, 16 * 4)
                if b >= 1:
                    pe.wait_ge(s_read, b)
                for t in range(NT):
                    last = nc.tensor.matmul(S_PS[:, t * P:(t + 1) * P], uT[:, b, t * P:(t + 1) * P],
                                            ow_sb[:], start=True, stop=True)
                last.then_inc(s_ps, 1)

            pe.wait_ge(sel_done, 1)
            pe.wait_ge(v_done, B)
            for b in range(B):
                hidden(HT * b)
                for i in range(HT):
                    if i + 1 < HT:
                        hidden(HT * b + i + 1)
                    expert_out(HT * b + i)
                    n = HT * b + i
                    if b == 0 and i % 2 == 1:
                        filter_spectrum(i // 2)
                    if b in FORTH and i % 2 == 1:
                        transform(KC * FORTH.index(b) + i // 2)
                    if b in BACK and i % 2 == 1:
                        transform_back(GB * BACK.index(b) + i // 2)
                    if n in YT_AT:
                        transpose_y(YT_AT.index(n))
                    if n in S_AT:
                        mixed(S_AT.index(n))
            transpose_y(B - 1)
            mixed(B - 1)


NAMES = ["L0_attn_x", "L0_attn_uv_w", "L0_attn_o_w", "L0_attn_rpe_pos_w", "L0_attn_rpe_ln_w",
         "L0_attn_rpe_ln_b", "L0_attn_rpe_fc_w", "L0_attn_rpe_out_ln_w", "L0_attn_rpe_out_ln_b",
         "L0_attn_rpe_out_w", "L0_ffn_W1", "L0_ffn_b1", "L0_ffn_W2", "L0_ffn_b2", "L0_ffn_Wr",
         "L0_ffn_br", "L0_ffn_gamma", "L0_ffn_beta"]


def kernel(**inputs):
    import concourse.bacc as bacc
    from concourse.bass_utils import run_bass_kernel_spmd

    nc = bacc.Bacc("TRN2", target_bir_lowering=False, num_devices=1)
    arrays = {f"in_{n}": np.ascontiguousarray(inputs[n]) for n in NAMES}
    arrays.update({f"table_{n}": a for n, a in shape_tables().items()})
    args = [nc.dram_tensor(n, a.shape, mybir.dt.from_np(a.dtype), kind="ExternalInput").ap()
            for n, a in arrays.items()]
    args.append(nc.dram_tensor("out_0_dram", (B, S, D), F32, kind="ExternalOutput").ap())
    build(nc, *args)
    r = run_bass_kernel_spmd(nc, [arrays], core_ids=[0])
    return r.results[0]["out_0_dram"]
```

```python
from contextlib import ExitStack

import numpy as np

import concourse.bass as bass
from concourse import mybir

ALU = mybir.AluOpType
ACT = mybir.ActivationFunctionType
AX = mybir.AxisListType.X
F32 = mybir.dt.float32
F32R = mybir.dt.float32r
U32 = mybir.dt.uint32

P = 128
B, S, D = 8, 512, 128
E, F, TOPK = 8, 512, 2
R, L = 32, 3
NT = S // P
NC = S // 2 // P
KC = S // P
LC = S // P
FC = F // P
RG = P // R
PW = 2 * S // RG
GB = 4
HT = TOPK * FC
EPS = 1e-5
GAMMA = 0.99

PROJECT_LAG = 6
STEPS = B + PROJECT_LAG
LOWER_AT = [4, 5, 6, 7, 8, 8, 9, 9]
LAYER_AT = [3, 7, 11]
ROUTER_AT = B
PRODUCT_AT, VARIANCE_AT, ROOT_AT, LAGS_AT = 0, 2, 4, 7
SPECTRUM_AT = [9, 9, 10, 11]
FORTH_AT = [14, 16, 18, 20, 30, 32, 34, 36]
BACK_AT = [22, 24, 26, 28, 42, 45, 50, 63]
YT_AT = [15, 19, 26, 33, 41, 49, 57]
S_AT = [25, 28, 31, 35, 45, 49, 58, 63]
TANH_AT = [21, 24, 31, 38, 46, 54, 64]
SPLIT_FROM = 5


def in_order(at):
    return [job for _, job in sorted((tile, (kind, first + n)) for (kind, first), tiles in at.items()
                                     for n, tile in enumerate(tiles))]


DVE_JOBS = in_order({
    ("w2", 0): [-1, 3, 12.5, 20.6, 29.4, 37.5, 44.3, 52.3],
    ("eps", L): [3], ("spread", L): [3.1], ("layer", L): [4.5],
    ("split", 2): [0, 0.1, 21.2, 21.6, 22, 22.2],
    ("products", 0): [14.1, 16, 18, 20, 30.1, 32, 34, 36.1],
    ("conv", 0): [23.6, 25.6, 27.6, 29.6, 43.9, 46.9, 51.9, 65],
    ("sum", 0): [15.5, 19.5, 26.3, 33.5, 42.1, 50.1, 58.1, 64.5],
    ("norm", 0): [16.7, 20.9, 27.8, 35, 43.3, 51.3, 59.3, 66],
    ("affine", B - 1): [67],
    ("result", 0): [26.7, 29.5, 32.4, 39.7, 48.5, 56, 63.5, 70],
    ("h", HT * SPLIT_FROM): [n - 0.8 for n in range(HT * SPLIT_FROM, HT * B)]})
POOL_JOBS = in_order({
    ("w1", 1): [2.5, 10, 18, 26, 33, 41, 49],
    ("cs", 0): [5], ("layer", L): [3],
    ("fold", 4): [9, 10, 21.3, 21.7],
    ("spectrum", 0): [14, 16, 18, 20, 30, 32, 34, 36.1],
    ("root", 0): [15.8, 19.8, 26.6, 33.9, 42.2, 50.2, 58.2, 64.9],
    ("affine", 0): [16.9, 21, 28, 35.5, 43.5, 51.5, 59.5]})
STORES = [[], [], [], [0, 1], [2, 3], [4], [5], [6, 7]]
RELOADS = [[0, 1, 2, 3], [], [], [4, 5], [6, 7], [], [], []]


def shape_tables():
    k = (np.arange(S) + 0.5) * (2 * np.pi / (2 * S))
    n = S / 2 - 0.5 - np.arange(S // 2)
    cs = np.stack([np.cos(np.outer(n, k)), np.sin(np.outer(n, k))])
    fwd = cs.reshape(2, NC, P, S).transpose(2, 1, 0, 3)
    inv = cs.transpose(2, 0, 1).reshape(KC, P, 2, S // 2).transpose(1, 0, 2, 3)
    lag = np.arange(S)
    decay = GAMMA ** lag / S * np.where(lag == 0, 0.5, 1.0)
    al = np.stack([np.cos(np.outer(lag, k)), -np.sin(np.outer(lag, k))]) * decay[None, :, None]
    al = al.reshape(2, LC, P, S).transpose(2, 1, 0, 3)
    same = np.kron(np.eye(RG), np.ones((R, R)))
    sign = np.zeros((P, 4))
    for g, (even, odd) in enumerate([(0, 1), (2, 3), (0, 1), (2, 3)]):
        sign[g * R:(g + 1) * R, even] = 1
        sign[g * R:(g + 1) * R, odd] = 1 if g < 2 else -1
    c128 = np.concatenate([np.eye(P), same, sign], axis=1)
    rep = np.tile(np.eye(R), (1, RG))
    half = np.arange(PW)
    pos = np.stack([half, half + PW, -half, -half - PW])
    mask4 = np.kron(np.eye(RG), np.ones((1, R)))
    c4 = np.concatenate([pos, mask4], axis=1)
    c8 = np.concatenate([np.tile(np.arange(E), (B, 1)), np.eye(B), np.ones((B, P))], axis=1)
    f = np.float32
    c32 = np.zeros((R, P + PW + P))
    c32[:, 0:P] = rep
    c32[0:RG, P:] = c4
    wide = np.zeros((P, c128.shape[1] + c8.shape[1]))
    wide[:, 0:c128.shape[1]] = c128
    wide[0:B, c128.shape[1]:] = c8
    return {"fwd": fwd.reshape(P, -1).astype(f), "inv": inv.reshape(P, -1).astype(f),
            "lag": al.reshape(P, -1).astype(f), "c128": wide.astype(f), "c32": c32.astype(f)}


def build(nc, x, uv_w, o_w, pos_w, ln_w, ln_b, fc_w, out_ln_w, out_ln_b, out_w,
          W1, b1, W2, b2, Wr, br, gamma, beta, t_fwd, t_inv, t_lag, t_c128, t_c32, out):
    with ExitStack() as ctx:
        def sb(name, shape, dt=F32):
            return ctx.enter_context(nc.sbuf_tensor(name, shape, dt))

        def sem(name):
            return ctx.enter_context(nc.semaphore(name))

        NX = NR = 4
        x_ring = sb("x_ring", [P, NX, NT, D])
        xn = sb("xn", [P, 2, NT, D])
        xT_hi = sb("xT_hi", [P, B, S], F32R)
        xT_lo = sb("xT_lo", [P, B, S], F32R)
        uT = sb("uT", [P, B, S])
        vt = sb("vt", [P, GB, 2, NC, D])
        pm = sb("pm", [P, 2, 2, NC, D])
        pm_hi = sb("pm_hi", [P, 2, NC, GB, D], F32R)
        pm_lo = sb("pm_lo", [P, 2, NC, GB, D], F32R)
        Y = sb("Y", [P, KC, 2, GB, D])
        prod = sb("prod", [P, 4, GB, D])
        A_sb = sb("A_sb", [P, KC, 2, D])
        cs_hi = sb("cs_hi", [P, NC, 2, S], F32R)
        cs_lo = sb("cs_lo", [P, NC, 2, S], F32R)
        inv_sb = sb("inv_sb", [P, KC, 2, S // 2])
        w1_raw = sb("w1_raw", [P, TOPK, F])
        w1_hi = sb("w1_hi", [P, 2, TOPK, F], F32R)
        w1_lo = sb("w1_lo", [P, 2, TOPK, F], F32R)
        w2_s = sb("w2_s", [P, 2, TOPK, FC, D])
        NH = 4
        h_ring = sb("h_ring", [P, NH, S])
        O_sb = sb("O_sb", [P, 2, S // 2])
        conv = sb("conv", [P, S])
        NY = 3
        yT = sb("yT", [P, NY, S])
        yb = sb("yb", [P, 2, NT, D])
        zb = sb("zb", [P, 2, NT, D])
        th = sb("th", [P, 2, NT, D])
        uvw_hi = sb("uvw_hi", [P, 2 * D], F32R)
        uvw_lo = sb("uvw_lo", [P, 2 * D], F32R)
        ow_sb = sb("ow_sb", [P, D])
        gam = sb("gam", [P, D])
        bet = sb("bet", [P, D])
        c128 = sb("c128", [P, 2 * P + 4 + E + B + P])
        stats = sb("stats", [P, NT, 6])
        mv = sb("mv", [P, B, NT, 2])
        rstd = sb("rstd", [P, B, NT])
        ystats = sb("ystats", [P, NT, 6])
        ymv = sb("ymv", [P, NT, 2])
        yrstd = sb("yrstd", [P, NT])
        xsum = sb("xsum", [P, B])
        xmean = sb("xmean", [P, B])
        wr_sb = sb("wr_sb", [P, E])
        br_sb = sb("br_sb", [B, E])
        br8 = br_sb[:]
        logit = sb("logit", [B, E])
        cw_sb = sb("cw_sb", [B, TOPK])
        b2_sb = sb("b2_sb", [E, D])
        ex = sb("ex", [B, E])
        rw = sb("rw", [B, E])
        top8 = sb("top8", [B, 8])
        rx = sb("rx", [B, 8])
        idx = sb("idx", [B, 8], U32)
        idxf = sb("idxf", [B, 8])
        onehot = sb("onehot", [B, 3, E])
        diag = sb("diag", [B, TOPK, B])
        selT = sb("selT", [E, 3, B])
        b1_sel = sb("b1_sel", [P, FC, TOPK, B])
        b2_mix = sb("b2_mix", [P, B])
        cw_all = sb("cw_all", [P, TOPK, B])
        lnT = sb("lnT", [P, 8])
        same32 = sb("same32", [P, P])
        minus_half = sb("minus_half", [P, 8])
        root = sb("root", [P, 8])
        layer_var = sb("layer_var", [P, 8])
        layer_r = sb("layer_r", [P, 8])

        def flat(t):
            return t.rearrange("p a b -> p (a b)")

        lag_sb = Y[:].rearrange("p a r b d -> p (a r b d)").rearrange("p (l r k) -> p l r k", l=LC, r=2)
        teto = prod[:, 0:2]
        cs_raw = inv_sb[:].rearrange("p a r i -> p (a r i)")
        uvw = O_sb[:].rearrange("p a i -> p (a i)")[:, 0:2 * D]
        b1_sb = conv[0:E, :]
        c32 = yT[:].rearrange("p a s -> p (a s)")[0:R, 0:P + PW + P]
        act, sq = flat(zb[:, 0])[:, 0:PW], flat(zb[:, 0])[:, PW:2 * PW]
        hc, nrm = flat(zb[:, 1])[:, 0:PW], flat(zb[:, 1])[:, PW:2 * PW]
        root_b = prod[:, 2].rearrange("p b d -> p (b d)")[:, 0:PW]
        fc_bd = th[:, 0, 0:L].rearrange("p l (g j) -> p l g j", g=RG)
        ow_v = th[:, 1]
        y0, y1 = flat(yb[:, 0]), flat(yb[:, 1])
        fcow, rep = y0[0:R, 0:L * R + D], c32[:, 0:P]
        rows8, l0 = y0[0:8, 384:384 + R], y0[0:RG, 416:416 + R]
        rows32, L0 = y1[0:8, 0:P], y1[0:RG, P:2 * P]
        fcc = y1[:, 256:256 + L * R].rearrange("p (l j) -> p l j", l=L)
        fmean, lmean, l0c = y1[:, 384:384 + L], y1[0:RG, 400:402], y1[0:RG, 416:416 + R]
        h_hi, h_lo = (t[:].rearrange("p a c b d -> p (a c b d)").rearrange("p (n s) -> p n s", n=NH)
                      for t in (pm_hi, pm_lo))
        w2_hi, w2_lo = (t[:].rearrange("p c r k -> p (c r k)")
                        .rearrange("p (a j c d) -> p a j c d", a=2, j=TOPK, c=FC) for t in (cs_hi, cs_lo))
        ident, same, sign = c128[:, 0:P], c128[:, P:2 * P], c128[:, 2 * P:2 * P + 4]
        pos, mask4 = c32[0:RG, P:P + PW], c32[0:RG, P + PW:]
        c8 = c128[0:B, 2 * P + 4:]
        nmax, esum, gap, e1, cw = rx[:, 1:2], rx[:, 2:3], rx[:, 4:5], rx[:, 5:6], cw_sb[:]
        xR_hi, xR_lo = (w1_x[:, 1].rearrange("p j (r n) -> p (j r) n", r=2) for w1_x in (w1_hi, w1_lo))
        iota8, ident8, ones8 = c8[:, 0:E], c8[:, E:E + B], c8[:, E + B:E + B + P]

        bank = [ctx.enter_context(nc.psum_tensor(f"bank{n}", [P, 512], F32)) for n in range(8)]
        T_PS = bank[0:2] + bank[6:8]
        H_PS = bank[0:2]
        OUT_PS, EO_PS = bank[2:4]
        SPARE_FROM = 5
        UV_PS = [bank[6:8] if b >= SPARE_FROM and (b - SPARE_FROM) % 2 == 0 else bank[2:4]
                 for b in range(B)]
        R_PS = S_PS = bank[4]
        Q_PS = YT_PS = bank[5]
        RT_PS, PICK_PS = bank[0:2]
        A_PS = V_RI = bank[6:8]

        x_in = [sem(f"x_in{n}") for n in range(NX)]
        consts_in = sem("consts_in")
        rpe_in = sem("rpe_in")
        uvw_in = sem("uvw_in")
        cs_in = sem("cs_in")
        lag_in = sem("lag_in")
        late_in, last_in, inv_in = sem("late_in"), sem("last_in"), sem("inv_in")
        w1_in, w2_in = sem("w1_in"), [sem("w2_in0"), sem("w2_in1")]
        out_done = [sem(f"out_done{n}") for n in range(NX)]
        dve_step, pool_step = sem("dve_step"), sem("pool_step")
        stats_done = sem("stats_done")
        xn_done = sem("xn_done")
        xT_ps, xhi_done, xrev_done, xlo_done = (
            sem("xT_ps"), sem("xhi_done"), sem("xrev_done"), sem("xlo_done"))
        uvw_hi_done, uvw_split = sem("uvw_hi_done"), sem("uvw_split")
        u_ps, v_ps, u_done, v_done = sem("u_ps"), sem("v_ps"), sem("u_done"), sem("v_done")
        pm_done, pm_split = sem("pm_done"), sem("pm_split")
        rpe_pe, rpe_ready = sem("rpe_pe"), sem("rpe_ready")
        hc_ps, sq_done, var_ps, nrm_done, act_done = (
            sem("hc_ps"), sem("sq_done"), sem("var_ps"), sem("nrm_done"), sem("act_done"))
        hc_done, varT_done, layer_r_done, root_b_done, root_ps = (
            sem("hc_done"), sem("varT_done"), sem("layer_r_done"), sem("root_b_done"), sem("root_ps"))
        ystats_done, yrstd_done = sem("ystats_done"), sem("yrstd_done")
        teto_ps, teto_done, A_ps, A_done = sem("teto_ps"), sem("teto_done"), sem("A_ps"), sem("A_done")
        cs_hi_done, cs_split = sem("cs_hi_done"), sem("cs_split")
        xmean_done, logit_ps, nmax_done, exp_done, gap_done, exp2_done = (
            sem("xmean_done"), sem("logit_ps"), sem("nmax_done"), sem("exp_done"), sem("gap_done"),
            sem("exp2_done"))
        idx_done, pick_done, pickT_ps, pickT_done, sel_ps, sel_done = (
            sem("idx_done"), sem("pick_done"), sem("pickT_ps"), sem("pickT_done"), sem("sel_ps"),
            sem("sel_done"))
        w1_hi_done, w1_split, w2_scaled = sem("w1_hi_done"), sem("w1_split"), sem("w2_scaled")
        h_ps, h_done, h_hi_done, h_split, w2_mm = (
            sem("h_ps"), sem("h_done"), sem("h_hi_done"), sem("h_split"), sem("w2_mm"))
        yT_done, y_ps, y_read = sem("yT_done"), sem("y_ps"), sem("y_read")
        rstd_done = sem("rstd_done")
        xn2_done, z_done, zg_done, th_done = sem("xn2_done"), sem("z_done"), sem("zg_done"), sem("th_done")
        s_ps, s_read, res_done = sem("s_ps"), sem("s_read"), sem("res_done")
        vre_ps, vim_ps, vre_read, vim_read, Y_done = (
            sem("vre_ps"), sem("vim_ps"), sem("vre_read"), sem("vim_read"), sem("Y_done"))
        eo_ps, O_done, eo_read, conv_done = sem("eo_ps"), sem("O_done"), sem("eo_read"), sem("conv_done")

        x_v = x.rearrange("b (t p) d -> b p t d", p=P)
        out_v = out.rearrange("b (t p) d -> b p t d", p=P)
        w2_v = W2.rearrange("e (c p) d -> e p c d", p=P)

        def bcast(ap, shape):
            return ap.broadcast_to(list(shape))

        block = ctx.enter_context(nc.Block())

        @block.sync
        def _(sp):
            def load_x(n):
                if n >= NX and n < B:
                    sp.wait_ge(xn_done, n - NX + 1)
                sp.dma_start(x_ring[:, n % NX], x_v[n]).then_inc(x_in[n % NX], 16)

            def reload_x(b):
                if b >= NX:
                    sp.wait_ge(out_done[b % NX], 16)
                sp.dma_start(x_ring[:, b % NX], x_v[b]).then_inc(x_in[b % NX], 16)

            load_x(0)
            load_x(1)
            sp.dma_start(uvw, uv_w).then_inc(uvw_in, 16)
            for b in range(2, B):
                load_x(b)
            for dst, src in ((wr_sb[:], Wr), (br8, br.partition_broadcast(B)),
                             (b1_sb, b1), (b2_sb[:], b2)):
                sp.dma_start(dst, src).then_inc(late_in, 16)
            sp.dma_start(cs_raw, t_fwd).then_inc(cs_in, 16)
            sp.dma_start(Y[:].rearrange("p a r b d -> p (a r b d)"), t_lag).then_inc(lag_in, 16)

            sp.wait_ge(idx_done, 1)

            def fetch_w1(b):
                if b >= 1:
                    sp.wait_ge(w1_split, TOPK * b)
                for j in range(TOPK):
                    e = sp.value_load(idx[b:b + 1, j:j + 1], min_val=0, max_val=E - 1)
                    sp.dma_start(w1_raw[:, j, :], W1[bass.ds(e, 1), :, :]
                                 .rearrange("e d f -> d (e f)")).then_inc(w1_in, 16)

            def fetch_w2(b):
                if b >= 2:
                    sp.wait_ge(w2_mm, HT * (b - 1))
                for j in range(TOPK):
                    e = sp.value_load(idx[b:b + 1, j:j + 1], min_val=0, max_val=E - 1)
                    sp.dma_start(w2_s[:, b % 2, j], w2_v[bass.ds(e, 1), :, :, :]
                                 .rearrange("e p c d -> p (e c) d")).then_inc(w2_in[b % 2], 16)

            fetch_w1(0)
            fetch_w2(0)
            fetch_w1(1)
            fetch_w2(1)
            for dst, src in ((ow_sb[:], o_w), (gam[:], gamma.partition_broadcast(P)),
                             (bet[:], beta.partition_broadcast(P))):
                sp.dma_start(dst, src).then_inc(last_in, 16)
            sp.wait_ge(xn_done, B)
            for b in range(B):
                if 1 <= b < B - 1:
                    fetch_w2(b + 1)
                if b + 2 < B:
                    fetch_w1(b + 2)
                for n in STORES[b]:
                    sp.wait_ge(res_done, n + 1)
                    sp.dma_start(out_v[n], x_ring[:, n % NX]).then_inc(out_done[n % NX], 16)
                for n in RELOADS[b]:
                    reload_x(n)
                if b == 0:
                    sp.wait_ge(cs_split, 1)
                    sp.dma_start(inv_sb[:].rearrange("p a r i -> p (a r i)"), t_inv).then_inc(inv_in, 16)
            for n in range(NX):
                sp.wait_ge(out_done[n], 16 * (B // NX))

        @block.scalar
        def _(act_e):
            act_e.dma_start(c128[:], t_c128).then_inc(consts_in, 16)
            for dst, src in ((c32, t_c32), (l0, pos_w.rearrange("a r -> (a r)").partition_broadcast(RG)),
                             (rows8[0:L], ln_w), (rows8[L:2 * L], ln_b),
                             (rows8[2 * L:2 * L + 1], out_ln_w.unsqueeze(0)),
                             (rows8[2 * L + 1:2 * L + 2], out_ln_b.unsqueeze(0)),
                             (fcow[:, 0:L * R].rearrange("f (l j) -> f l j", l=L),
                              fc_w.rearrange("l f j -> f l j")),
                             (fcow[:, L * R:L * R + D], out_w)):
                act_e.dma_start(dst, src).then_inc(rpe_in, 16)

            def xn_hi(b):
                act_e.wait_ge(xT_ps, b + 1)
                nc.scalar.activation(xT_hi[:, b, :], T_PS[b % NR][:], ACT.Copy,
                                     accum_out=xsum[:, b:b + 1]).then_inc(xhi_done, 1)

            def xn_hi_reversed(b):
                if b >= NR:
                    act_e.wait_ge(v_ps, b - NR + 1)
                nc.scalar.activation(xR_hi[:, b % NR], T_PS[b % NR][:, S - 1:S // 2 - 1:-1],
                                     ACT.Copy).then_inc(xrev_done, 1)

            def layer_square(n):
                act_e.wait_ge(hc_ps, n + 1)
                nc.scalar.activation(sq, R_PS[:, 0:PW], ACT.Square).then_inc(sq_done, 1)
                nc.scalar.activation(hc, R_PS[:, 0:PW], ACT.Copy).then_inc(hc_done, 1)

            def layer_silu(n):
                scale, bias = (n, L + n) if n < L else (2 * L, 2 * L + 1)
                act_e.wait_ge(nrm_done, n + 1)
                nc.scalar.activation(act, nrm, ACT.Silu, bias=lnT[:, bias:bias + 1],
                                     scale=lnT[:, scale:scale + 1]).then_inc(act_done, 1)

            def router_exponentials():
                act_e.wait_ge(nmax_done, 1)
                nc.scalar.activation(ex[:], logit[:], ACT.Exp, bias=nmax,
                                     accum_out=esum).then_inc(exp_done, 1)
                act_e.wait_ge(gap_done, 1)
                nc.scalar.activation(e1, gap, ACT.Exp).then_inc(exp2_done, 1)

            def silu_uv(b):
                act_e.wait_ge(u_ps, b + 1)
                nc.scalar.activation(uT[:, b, :], UV_PS[b][0][:], ACT.Silu).then_inc(u_done, 1)
                act_e.wait_ge(v_ps, b + 1)
                if b >= GB:
                    act_e.wait_ge(pm_done, b - GB + 1)
                nc.scalar.activation(vt[:, b % GB].rearrange("p r c d -> p (r c d)"), UV_PS[b][1][:],
                                     ACT.Silu).then_inc(v_done, 1)

            def w1_upper(b):
                act_e.wait_ge(w1_in, 16 * TOPK * (b + 1))
                if b == 1:
                    act_e.wait_ge(v_ps, B)
                if b >= 2:
                    act_e.wait_ge(h_ps, HT * (b - 1))
                for j in range(TOPK):
                    nc.scalar.activation(w1_hi[:, b % 2, j], w1_raw[:, j], ACT.Copy).then_inc(w1_hi_done, 1)

            act_e.wait_ge(uvw_in, 16)
            nc.scalar.activation(uvw_hi[:], uvw, ACT.Copy).then_inc(uvw_hi_done, 1)
            for b in range(STEPS):
                for n in (n for n in range(B) if LOWER_AT[n] == b):
                    xn_hi_reversed(n)
                if b - 1 in LAYER_AT:
                    layer_square(LAYER_AT.index(b - 1))
                if PROJECT_LAG <= b:
                    silu_uv(b - PROJECT_LAG)
                if b - 3 in LAYER_AT:
                    layer_silu(LAYER_AT.index(b - 3))
                if b == ROUTER_AT + 2:
                    router_exponentials()
                if 1 <= b <= B:
                    xn_hi(b - 1)
                if b == STEPS - 2:
                    w1_upper(0)

            def cs_upper():
                act_e.wait_ge(cs_in, 16)
                nc.scalar.activation(cs_hi[:].rearrange("p c r k -> p (c r k)"), cs_raw,
                                     ACT.Copy).then_inc(cs_hi_done, 1)

            def lag_rows():
                act_e.wait_ge(teto_ps, 1)
                for n in range(2):
                    nc.scalar.activation(teto[:, n].rearrange("p q d -> p (q d)"),
                                         A_PS[n][:], ACT.Copy).then_inc(teto_done, 1)

            def filter_read():
                act_e.wait_ge(A_ps, 1)
                for m in range(2):
                    nc.scalar.activation(A_sb[:, 2 * m:2 * m + 2].rearrange("p a r d -> p (a r d)"),
                                         A_PS[m][:], ACT.Copy).then_inc(A_done, 1)

            def gelu(n):
                b, j, c = n // HT, n % HT // FC, n % FC
                act_e.wait_ge(h_ps, n + 1)
                if n >= NH:
                    act_e.wait_ge(w2_mm, n - NH + 1)
                nc.scalar.activation(h_ring[:, n % NH], H_PS[n % 2][:], ACT.Gelu,
                                     bias=b1_sel[:, c, j, b:b + 1]).then_inc(h_done, 1)
                if b >= SPLIT_FROM:
                    if n == HT * SPLIT_FROM:
                        act_e.wait_ge(vim_ps, KC * B // GB)
                    nc.scalar.activation(h_hi[:, n % NH], H_PS[n % 2][:], ACT.Gelu,
                                         bias=b1_sel[:, c, j, b:b + 1]).then_inc(h_hi_done, 1)

            def experts_out(b):
                act_e.wait_ge(w2_mm, HT * (b + 1))
                if b >= NY:
                    act_e.wait_ge(y_ps, b - NY + 1)
                nc.scalar.activation(yT[:, b % NY], OUT_PS[:], ACT.Identity,
                                     bias=b2_mix[:, b:b + 1]).then_inc(yT_done, 1)

            def odd_part(b):
                act_e.wait_ge(eo_ps, b + 1)
                if b >= 2:
                    act_e.wait_ge(eo_read, b - 1)
                nc.scalar.activation(O_sb[:, b % 2], EO_PS[:, S // 2:S], ACT.Copy).then_inc(O_done, 1)

            def gate_tanh(b):
                act_e.wait_ge(zg_done, b + 1)
                if b >= 2:
                    act_e.wait_ge(res_done, b - 1)
                nc.scalar.activation(th[:, b % 2], zb[:, b % 2], ACT.Tanh, scale=0.5).then_inc(th_done, 1)

            act_e.wait_ge(sel_done, 1)
            layer_silu(L - 1)
            for n in range(HT * B + 2):
                if n < HT * B:
                    gelu(n)
                    if n % HT == 2 and n // HT + 1 < B:
                        w1_upper(n // HT + 1)
                if n == 3:
                    cs_upper()
                if n % HT == 1 and n >= HT:
                    experts_out(n // HT - 1)
                if n - 2 == PRODUCT_AT:
                    layer_square(L)
                if n - 2 == ROOT_AT:
                    layer_silu(L)
                if n - 2 == LAGS_AT:
                    lag_rows()
                if n - 2 == SPECTRUM_AT[-1]:
                    filter_read()
                if n - 2 in BACK_AT:
                    odd_part(BACK_AT.index(n - 2))
                if n in TANH_AT:
                    gate_tanh(TANH_AT.index(n))
            gate_tanh(B - 1)

        @block.gpsimd
        def _(pool):
            steps = [0]

            def step(ins):
                steps[0] += 1
                ins.then_inc(pool_step, 1)
                pool.wait_ge(pool_step, steps[0])

            def inverse_root(out_r, var, n):
                step(nc.gpsimd.tensor_scalar(root[:, 0:n], var, EPS, None, ALU.add))
                return nc.gpsimd.tensor_tensor(out_r, root[:, 0:n], minus_half[:, 0:n], ALU.pow)

            def gate_root(b):
                pool.wait_ge(ystats_done, b + 1)
                pool.wait_ge(*((rstd_done, B) if b == 0 else (yrstd_done, b)))
                inverse_root(yrstd[:], ymv[:, :, 1], NT).then_inc(yrstd_done, 1)

            def layer_root(n):
                pool.wait_ge(varT_done, n + 1)
                if n >= 1:
                    pool.wait_ge(layer_r_done, n)
                nc.gpsimd.tensor_tensor(layer_r[:], layer_var[:], minus_half[:], ALU.pow).then_inc(
                    layer_r_done, 1)

            def rows_root(b):
                pool.wait_ge(stats_done, b + 1)
                if b >= 1:
                    pool.wait_ge(rstd_done, b)
                inverse_root(rstd[:, b], mv[:, b, :, 1], NT).then_inc(rstd_done, 1)

            def fold(b):
                pool.wait_ge(v_done, b + 1)
                if b >= 2:
                    pool.wait_ge(pm_split, b - 1)
                nc.gpsimd.tensor_tensor(pm[:, b % 2, 0], vt[:, b % GB, 0], vt[:, b % GB, 1], ALU.add)
                nc.gpsimd.tensor_tensor(pm[:, b % 2, 1], vt[:, b % GB, 0], vt[:, b % GB, 1],
                                        ALU.subtract).then_inc(pm_done, 1)

            def spectrum(q):
                pool.wait_ge(vim_read, q + 1)
                if q == KC:
                    pool.wait_ge(eo_ps, GB)
                nc.gpsimd.tensor_tensor(Y[:, q % KC, 0], prod[:, 0], prod[:, 2], ALU.subtract)
                nc.gpsimd.tensor_tensor(Y[:, q % KC, 1], prod[:, 1], prod[:, 3],
                                        ALU.add).then_inc(Y_done, 1)

            def w1_lower(b):
                for j in range(TOPK):
                    pool.wait_ge(w1_hi_done, TOPK * b + j + 1)
                    nc.gpsimd.tensor_tensor(w1_lo[:, b % 2, j], w1_raw[:, j], w1_hi[:, b % 2, j],
                                            ALU.subtract).then_inc(w1_split, 1)

            def gate_affine(b):
                if b == 0:
                    pool.wait_ge(last_in, 16 * 3)
                pool.wait_ge(z_done, b + 1)
                step(nc.gpsimd.tensor_tensor(zb[:, b % 2], zb[:, b % 2],
                                             bcast(gam[:].unsqueeze(1), [P, NT, D]), ALU.mult))
                nc.gpsimd.tensor_tensor(zb[:, b % 2], zb[:, b % 2],
                                        bcast(bet[:].unsqueeze(1), [P, NT, D]),
                                        ALU.add).then_inc(zg_done, 1)

            def cs_lower():
                pool.wait_ge(cs_hi_done, 1)
                nc.gpsimd.tensor_tensor(cs_lo[:].rearrange("p c r k -> p (c r k)"), cs_raw,
                                        cs_hi[:].rearrange("p c r k -> p (c r k)"),
                                        ALU.subtract).then_inc(cs_split, 1)

            step(nc.gpsimd.memset(minus_half[:], -0.5))
            for b in range(STEPS):
                if b < B:
                    rows_root(b)
                if b == 3:
                    pool.wait_ge(uvw_hi_done, 1)
                    nc.gpsimd.tensor_tensor(uvw_lo[:], uvw, uvw_hi[:], ALU.subtract).then_inc(uvw_split, 1)
                if PROJECT_LAG + 1 <= b < PROJECT_LAG + 1 + GB:
                    fold(b - PROJECT_LAG - 1)
                if b == STEPS - 2:
                    w1_lower(0)
                if b - 1 in LAYER_AT:
                    layer_root(LAYER_AT.index(b - 1))
            jobs = {"w1": w1_lower, "layer": layer_root, "spectrum": spectrum, "fold": fold, "root": gate_root,
                    "affine": gate_affine}
            for what, n in POOL_JOBS:
                if what == "cs":
                    cs_lower()
                else:
                    jobs[what](n)

        @block.vector
        def _(dve):
            steps = [0]

            def step(ins):
                steps[0] += 1
                ins.then_inc(dve_step, 1)
                dve.wait_ge(dve_step, steps[0])

            def row_stats(src, st, out_mv):
                for t in range(NT):
                    last = nc.vector.bn_stats(st[:, t], src[:, t])
                step(last)
                for t in range(NT):
                    last = nc.vector.bn_aggr(out_mv[:, t], st[:, t])
                return last

            def x_stats(b):
                dve.wait_ge(x_in[b % NX], 16 * (b // NX + 1))
                if b >= 1:
                    dve.wait_ge(stats_done, b)
                row_stats(x_ring[:, b % NX], stats, mv[:, b]).then_inc(stats_done, 1)

            def normalize(b):
                dve.wait_ge(rstd_done, b + 1)
                if b >= 2:
                    dve.wait_ge(xT_ps, b - 1)
                for t in range(NT):
                    last = nc.vector.tensor_scalar(xn[:, b % 2, t], x_ring[:, b % NX, t],
                                                   mv[:, b, t, 0:1], rstd[:, b, t:t + 1],
                                                   ALU.subtract, ALU.mult)
                last.then_inc(xn_done, 1)

            def normalize_again(b):
                dve.wait_ge(x_in[b % NX], 16 * (B // NX + b // NX + 1))
                for t in range(NT):
                    last = nc.vector.tensor_scalar(yb[:, b % 2, t], x_ring[:, b % NX, t],
                                                   mv[:, b, t, 0:1], rstd[:, b, t:t + 1],
                                                   ALU.subtract, ALU.mult)
                last.then_inc(xn2_done, 1)

            def w2_scale(b):
                dve.wait_ge(w2_in[b % 2], 16 * TOPK * (b // 2 + 1))
                if b == 0:
                    dve.wait_ge(sel_done, 1)
                if b < SPLIT_FROM:
                    for j in range(TOPK):
                        last = nc.vector.tensor_scalar(w2_s[:, b % 2, j], w2_s[:, b % 2, j],
                                                       cw_all[:, j, b:b + 1], None, ALU.mult)
                else:
                    if b == SPLIT_FROM:
                        dve.wait_ge(vim_ps, KC * B // GB)
                    for j in range(TOPK):
                        last = nc.vector.tensor_scalar(w2_hi[:, b % 2, j], w2_s[:, b % 2, j],
                                                       cw_all[:, j, b:b + 1], None, ALU.mult)
                    step(last)
                    for j in range(TOPK):
                        last = nc.vector.scalar_tensor_tensor(
                            out=w2_lo[:, b % 2, j], in0=w2_s[:, b % 2, j], scalar=cw_all[:, j, b:b + 1],
                            in1=w2_hi[:, b % 2, j], op0=ALU.mult, op1=ALU.subtract)
                last.then_inc(w2_scaled, 1)

            def h_lower(n):
                dve.wait_ge(h_hi_done, n - HT * SPLIT_FROM + 1)
                if n == HT * SPLIT_FROM:
                    dve.wait_ge(vim_ps, KC * B // GB)
                nc.vector.tensor_tensor(h_lo[:, n % NH], h_ring[:, n % NH], h_hi[:, n % NH],
                                        ALU.subtract).then_inc(h_split, 1)

            def xn_lo(b):
                dve.wait_ge(xrev_done, b + 1)
                nc.vector.tensor_tensor(xT_lo[:, b, :], T_PS[b % NR][:], xT_hi[:, b, :],
                                        ALU.subtract)
                if b >= NR:
                    dve.wait_ge(v_ps, b - NR + 1)
                nc.vector.tensor_tensor(xR_lo[:, b % NR], T_PS[b % NR][:, S - 1:S // 2 - 1:-1],
                                        xR_hi[:, b % NR], ALU.subtract).then_inc(xlo_done, 1)

            def split_fold(b):
                dve.wait_ge(pm_done, b + 1)
                if b == GB:
                    dve.wait_ge(vim_ps, KC)
                step(nc.vector.tensor_copy(pm_hi[:, :, :, b % GB, :], pm[:, b % 2]))
                nc.vector.tensor_tensor(pm_lo[:, :, :, b % GB, :], pm[:, b % 2],
                                        pm_hi[:, :, :, b % GB, :], ALU.subtract).then_inc(pm_split, 1)

            def layer_eps(n):
                dve.wait_ge(var_ps, n + 1)
                nc.vector.tensor_scalar(layer_var[:], Q_PS[:, 0:8], EPS, None, ALU.add).then_inc(varT_done, 1)

            def layer_spread(n):
                dve.wait_ge(layer_r_done, n + 1)
                nc.vector.tensor_copy(root_b.rearrange("p (q j) -> p q j", j=R),
                                      bcast(layer_r[:].unsqueeze(2), [P, 8, R])).then_inc(root_b_done, 1)

            def layer_norm(n):
                dve.wait_ge(root_ps, n + 1)
                dve.wait_ge(hc_done, n + 1)
                nc.vector.tensor_tensor(nrm, Q_PS[:, PW:2 * PW], hc, ALU.mult).then_inc(nrm_done, 1)

            def position_weights():
                dve.wait_ge(rpe_in, 16 * 8)
                dve.wait_ge(consts_in, 16)
                nc.vector.tensor_copy(rows32.rearrange("r (g j) -> r g j", g=RG),
                                      bcast(rows8.unsqueeze(1), [8, RG, R]))
                step(nc.vector.tensor_reduce(lmean[:, 0:1], l0, AX, ALU.add))
                step(nc.vector.tensor_scalar(lmean[:, 1:2], lmean[:, 0:1], -1.0 / R, None, ALU.mult))
                step(nc.vector.tensor_scalar(l0c, l0, lmean[:, 1:2], None, ALU.add))
                nc.vector.tensor_tensor(L0.rearrange("r (g j) -> r g j", g=RG),
                                        bcast(l0c.unsqueeze(1), [RG, RG, R]),
                                        mask4.rearrange("r (g j) -> r g j", g=RG), ALU.mult)
                nc.vector.tensor_scalar(same32[:], same, 1.0 / R, None, ALU.mult).then_inc(rpe_ready, 1)

            def position_matrices():
                dve.wait_ge(rpe_pe, 1)
                nc.vector.tensor_copy(lnT[:], R_PS[:, 0:8])
                fc_ps = R_PS[:, P:P + L * R].rearrange("p (l j) -> p l j", l=L)
                step(nc.vector.tensor_reduce(fmean, fc_ps, AX, ALU.add))
                step(nc.vector.tensor_scalar(fmean, fmean, -1.0 / R, None, ALU.mult))
                step(nc.vector.tensor_tensor(fcc, fc_ps, bcast(fmean.unsqueeze(2), [P, L, R]), ALU.add))
                for n in range(L):
                    nc.vector.tensor_tensor(fc_bd[:, n], bcast(fcc[:, n].unsqueeze(1), [P, RG, R]),
                                            same.rearrange("p (g j) -> p g j", g=RG), ALU.mult)
                nc.vector.tensor_tensor(ow_v, bcast(R_PS[:, P + L * R:P + L * R + D].unsqueeze(1), [P, 4, D]),
                                        bcast(sign.unsqueeze(2), [P, 4, D]), ALU.mult).then_inc(rpe_ready, 1)

            def router_mean():
                dve.wait_ge(xhi_done, B)
                nc.vector.tensor_scalar(xmean[:], xsum[:], 1.0 / S, None, ALU.mult).then_inc(xmean_done, 1)

            def router_logits():
                dve.wait_ge(logit_ps, 1)
                step(nc.vector.tensor_tensor(logit[:], RT_PS[0:B, 0:E], br8, ALU.add))
                step(nc.vector.tensor_reduce(rx[:, 0:1], logit[:], AX, ALU.max))
                nc.vector.tensor_scalar(nmax, rx[:, 0:1], -1.0, None, ALU.mult).then_inc(nmax_done, 1)

            def router_top():
                dve.wait_ge(exp_done, 1)
                step(nc.vector.reciprocal(rx[:, 3:4], esum))
                step(nc.vector.tensor_scalar(rw[:], ex[:], rx[:, 3:4], None, ALU.mult))
                step(nc.vector.max(top8[:], rw[:]))
                nc.vector.tensor_tensor(gap, top8[:, 1:2], top8[:, 0:1], ALU.subtract).then_inc(gap_done, 1)
                nc.vector.max_index(idx[:], top8[:], rw[:]).then_inc(idx_done, 1)
                dve.wait_ge(idx_done, 1)
                step(nc.vector.tensor_copy(idxf[:], idx[:]))
                for j in range(TOPK):
                    nc.vector.tensor_scalar(onehot[:, j], iota8, idxf[:, j:j + 1], None, ALU.is_equal)

            def router_mix():
                dve.wait_ge(exp2_done, 1)
                step(nc.vector.tensor_scalar(rx[:, 6:7], e1, 1.0, None, ALU.add))
                step(nc.vector.reciprocal(cw[:, 0:1], rx[:, 6:7]))
                step(nc.vector.tensor_tensor(cw[:, 1:2], e1, cw[:, 0:1], ALU.mult))
                for j in range(TOPK):
                    nc.vector.tensor_scalar(diag[:, j], ident8, cw[:, j:j + 1], None, ALU.mult)
                step(nc.vector.tensor_scalar(ex[:], onehot[:, 0], cw[:, 0:1], None, ALU.mult))
                nc.vector.scalar_tensor_tensor(out=onehot[:, 2], in0=onehot[:, 1], scalar=cw[:, 1:2],
                                               in1=ex[:], op0=ALU.mult, op1=ALU.add).then_inc(pick_done, 1)

            def router_picks():
                dve.wait_ge(pickT_ps, 1)
                nc.vector.tensor_copy(selT[:].rearrange("e q b -> e (q b)"),
                                      RT_PS[0:E, 64:64 + 3 * B]).then_inc(pickT_done, 1)
                dve.wait_ge(sel_ps, 1)
                n1 = FC * TOPK * B
                o = 64 + n1
                nc.vector.tensor_copy(b1_sel[:].rearrange("p c j b -> p (c j b)"), PICK_PS[:, 64:64 + n1])
                nc.vector.tensor_copy(b2_mix[:], PICK_PS[:, o:o + B])
                nc.vector.tensor_copy(cw_all[:].rearrange("p j b -> p (j b)"),
                                      PICK_PS[:, o + B:o + 3 * B]).then_inc(sel_done, 1)

            for b in range(STEPS):
                if b < B:
                    x_stats(b)
                if 1 <= b <= B:
                    normalize(b - 1)
                if b - 2 in LAYER_AT:
                    layer_spread(LAYER_AT.index(b - 2))
                if b == ROUTER_AT + 1:
                    router_logits()
                for n in (n for n in range(B) if LOWER_AT[n] == b):
                    xn_lo(n)
                if b == LAYER_AT[0] - 1:
                    position_weights()
                if b == LAYER_AT[0]:
                    position_matrices()
                if b == ROUTER_AT:
                    router_mean()
                if b == ROUTER_AT + 4:
                    router_picks()
                if b - 2 in LAYER_AT:
                    layer_norm(LAYER_AT.index(b - 2))
                if PROJECT_LAG + 2 <= b < PROJECT_LAG + 4:
                    split_fold(b - PROJECT_LAG - 2)
                if b == ROUTER_AT + 2:
                    router_top()
                    router_mix()
                if b - 1 in LAYER_AT:
                    layer_eps(LAYER_AT.index(b - 1))

            def products(q):
                kc = q % KC
                a_re = bcast(A_sb[:, kc, 0].unsqueeze(1), [P, GB, D])
                a_im = bcast(A_sb[:, kc, 1].unsqueeze(1), [P, GB, D])
                v_re = V_RI[0][:].rearrange("p (b d) -> p b d", b=GB)
                v_im = V_RI[1][:].rearrange("p (b d) -> p b d", b=GB)
                if q == 0:
                    dve.wait_ge(A_done, 2)
                if q >= 1:
                    dve.wait_ge(Y_done, q)
                dve.wait_ge(vre_ps, q + 1)
                nc.vector.tensor_tensor(prod[:, 0], v_re, a_re, ALU.mult)
                nc.vector.tensor_tensor(prod[:, 1], v_re, a_im, ALU.mult).then_inc(vre_read, 1)
                dve.wait_ge(vim_ps, q + 1)
                nc.vector.tensor_tensor(prod[:, 2], v_im, a_im, ALU.mult)
                nc.vector.tensor_tensor(prod[:, 3], v_im, a_re, ALU.mult).then_inc(vim_read, 1)

            def convolved(b):
                dve.wait_ge(O_done, b + 1)
                if b >= 1:
                    dve.wait_ge(conv_done, b)
                nc.vector.tensor_tensor(conv[:, 0:S // 2], EO_PS[:, 0:S // 2], O_sb[:, b % 2], ALU.add)
                nc.vector.tensor_tensor(conv[:, S - 1:S // 2 - 1:-1], EO_PS[:, 0:S // 2], O_sb[:, b % 2],
                                        ALU.subtract).then_inc(eo_read, 1)
                dve.wait_ge(eo_read, b + 1)
                nc.vector.tensor_tensor(uT[:, b, :], uT[:, b, :], conv[:], ALU.mult).then_inc(conv_done, 1)

            def gate_sum(b):
                normalize_again(b)
                dve.wait_ge(y_ps, b + 1)
                dve.wait_ge(xn2_done, b + 1)
                nc.vector.tensor_tensor(yb[:, b % 2].rearrange("p t d -> p (t d)"), YT_PS[:],
                                        yb[:, b % 2].rearrange("p t d -> p (t d)"),
                                        ALU.add).then_inc(y_read, 1)
                dve.wait_ge(y_read, b + 1)
                if b >= 1:
                    dve.wait_ge(z_done, b)
                row_stats(yb[:, b % 2], ystats, ymv).then_inc(ystats_done, 1)

            def gate_norm(b):
                dve.wait_ge(yrstd_done, b + 1)
                for t in range(NT):
                    last = nc.vector.tensor_scalar(zb[:, b % 2, t], yb[:, b % 2, t], ymv[:, t, 0:1],
                                                   yrstd[:, t:t + 1], ALU.subtract, ALU.mult)
                last.then_inc(z_done, 1)

            def gate_affine(b):
                dve.wait_ge(z_done, b + 1)
                step(nc.vector.tensor_tensor(zb[:, b % 2], zb[:, b % 2],
                                             bcast(gam[:].unsqueeze(1), [P, NT, D]), ALU.mult))
                nc.vector.tensor_tensor(zb[:, b % 2], zb[:, b % 2],
                                        bcast(bet[:].unsqueeze(1), [P, NT, D]),
                                        ALU.add).then_inc(zg_done, 1)

            def result(b):
                w = th[:, b % 2]
                dve.wait_ge(th_done, b + 1)
                step(nc.vector.scalar_tensor_tensor(out=w, in0=w, scalar=1.0, in1=zb[:, b % 2],
                                                    op0=ALU.add, op1=ALU.mult))
                dve.wait_ge(s_ps, b + 1)
                nc.vector.tensor_tensor(w, S_PS[:].rearrange("p (t d) -> p t d", t=NT), w,
                                        ALU.mult).then_inc(s_read, 1)
                dve.wait_ge(s_read, b + 1)
                nc.vector.scalar_tensor_tensor(out=x_ring[:, b % NX], in0=w, scalar=0.5,
                                               in1=x_ring[:, b % NX], op0=ALU.mult,
                                               op1=ALU.add).then_inc(res_done, 1)

            jobs = {"w2": w2_scale, "eps": layer_eps, "spread": layer_spread, "layer": layer_norm,
                    "h": h_lower, "products": products, "conv": convolved, "split": split_fold,
                    "sum": gate_sum, "norm": gate_norm, "affine": gate_affine, "result": result}
            for what, n in DVE_JOBS:
                jobs[what](n)

        @block.tensor
        def _(pe):
            def three(out_ps, w_hi, w_lo, m_hi, m_lo, start=True, stop=True):
                nc.tensor.matmul(out_ps, w_hi, m_hi, start=start, stop=False)
                nc.tensor.matmul(out_ps, w_hi, m_lo, start=False, stop=False)
                return nc.tensor.matmul(out_ps, w_lo, m_hi, start=False, stop=stop)

            def transpose_x(b):
                pe.wait_ge(xn_done, b + 1)
                if b == 0:
                    pe.wait_ge(consts_in, 16)
                if b >= NR:
                    pe.wait_ge(xlo_done, b - NR + 1)
                for t in range(NT):
                    last = nc.tensor.transpose(T_PS[b % NR][:, t * P:(t + 1) * P], xn[:, b % 2, t], ident)
                last.then_inc(xT_ps, 1)

            def project(b):
                u_ps_b, v_ps_b = UV_PS[b]
                pe.wait_ge(xlo_done, B if b >= SPARE_FROM else b + 1)
                if b == 0:
                    pe.wait_ge(uvw_split, 1)
                last_use = b - 1 if b < SPARE_FROM else b - 2
                if last_use >= 0:
                    pe.wait_ge(u_done, last_use + 1)
                three(u_ps_b[:], uvw_hi[:, 0:D], uvw_lo[:, 0:D], xT_hi[:, b], xT_lo[:, b]).then_inc(u_ps, 1)
                if last_use >= 0:
                    pe.wait_ge(v_done, last_use + 1)
                for r in range(2):
                    for c in range(NC):
                        rows = slice(c * P, (c + 1) * P)
                        hi, lo = (xT_hi[:, b, rows], xT_lo[:, b, rows]) if r == 0 else \
                            (xR_hi[:, b % NR, rows], xR_lo[:, b % NR, rows])
                        o = (r * NC + c) * D
                        last = three(v_ps_b[:, o:o + D], hi, lo,
                                     uvw_hi[:, D:2 * D], uvw_lo[:, D:2 * D])
                last.then_inc(v_ps, 1)

            def layer_product(n):
                if n == 0:
                    pe.wait_ge(rpe_ready, 2)
                    nc.tensor.matmul(R_PS[:, 0:PW], L0, pos, start=True, stop=True).then_inc(hc_ps, 1)
                else:
                    pe.wait_ge(act_done, n)
                    nc.tensor.matmul(R_PS[:, 0:PW], fc_bd[:, n - 1].rearrange("p g j -> p (g j)"), act,
                                     start=True, stop=True).then_inc(hc_ps, 1)

            def layer_variance(n):
                pe.wait_ge(sq_done, n + 1)
                for cc in range(2):
                    last = nc.tensor.matmul(Q_PS[:, cc * RG:(cc + 1) * RG], sq[:, cc * P:(cc + 1) * P],
                                            same32[:, 0:P:R], start=True, stop=True)
                last.then_inc(var_ps, 1)

            def layer_root_back(n):
                pe.wait_ge(root_b_done, n + 1)
                for cc in range(2):
                    last = nc.tensor.transpose(Q_PS[:, PW + cc * P:PW + (cc + 1) * P],
                                               root_b[:, cc * P:(cc + 1) * P], ident)
                last.then_inc(root_ps, 1)

            def even_odd_lags():
                pe.wait_ge(act_done, L + 1)
                for cc in range(2):
                    last = nc.tensor.matmul(A_PS[cc][:], act[:, cc * P:(cc + 1) * P],
                                            ow_v.rearrange("p q d -> p (q d)"), start=True, stop=True)
                last.then_inc(teto_ps, 1)

            def filter_spectrum(kc):
                if kc == 0:
                    pe.wait_ge(teto_done, 2)
                    pe.wait_ge(lag_in, 16)
                for ri in range(2):
                    o = (kc % 2) * 2 * D + ri * D
                    for lc in range(LC):
                        last = nc.tensor.matmul(A_PS[kc // 2][:, o:o + D],
                                                lag_sb[:, lc, ri, kc * P:(kc + 1) * P],
                                                teto[:, lc % 2, 2 * (lc // 2) + ri],
                                                start=(lc == 0), stop=(lc == LC - 1))
                if kc == KC - 1:
                    last.then_inc(A_ps, 1)

            def router_logits():
                pe.wait_ge(xmean_done, 1)
                pe.wait_ge(late_in, 16 * 4)
                pe.wait_ge(xlo_done, B - NR + 1)
                nc.tensor.matmul(RT_PS[0:B, 0:E], xmean[:], wr_sb[:], start=True, stop=True).then_inc(logit_ps, 1)

            def router_picks():
                pe.wait_ge(pick_done, 1)
                pe.wait_ge(xlo_done, B - NR + 2)
                for q in range(3):
                    last = nc.tensor.transpose(RT_PS[0:E, 64 + q * B:64 + (q + 1) * B], onehot[:, q], ident8)
                last.then_inc(pickT_ps, 1)
                pe.wait_ge(pickT_done, 1)
                picks = selT[:, 0:TOPK].rearrange("e j b -> e (j b)")
                w = TOPK * B
                for c in range(FC):
                    nc.tensor.matmul(PICK_PS[:, 64 + c * w:64 + (c + 1) * w], b1_sb[:, c * P:(c + 1) * P], picks,
                                     start=True, stop=True)
                o = 64 + FC * w
                nc.tensor.matmul(PICK_PS[:, o:o + B], b2_sb[:], selT[:, 2], start=True, stop=True)
                nc.tensor.matmul(PICK_PS[:, o + B:o + B + w], ones8, diag[:].rearrange("b j c -> b (j c)"),
                                 start=True, stop=True).then_inc(sel_ps, 1)

            for b in range(STEPS):
                if b == LAYER_AT[0]:
                    pe.wait_ge(rpe_ready, 1)
                    nc.tensor.transpose(R_PS[:, 0:8], rows32, ident[0:8, 0:8])
                    nc.tensor.matmul(R_PS[:, P:P + L * R + D], rep, fcow, start=True,
                                     stop=True).then_inc(rpe_pe, 1)
                if PROJECT_LAG <= b:
                    project(b - PROJECT_LAG)
                if b == ROUTER_AT + 4:
                    router_picks()
                if b - 1 in LAYER_AT:
                    layer_variance(LAYER_AT.index(b - 1))
                if 1 <= b <= B:
                    transpose_x(b - 1)
                if b - 2 in LAYER_AT:
                    layer_root_back(LAYER_AT.index(b - 2))
                if b == ROUTER_AT:
                    router_logits()
                if b in LAYER_AT:
                    layer_product(LAYER_AT.index(b))

            def hidden(n):
                b, j, c = n // HT, n % HT // FC, n % FC
                if n % FC == 0:
                    pe.wait_ge(w1_split, n // FC + 1)
                if n >= 2:
                    pe.wait_ge(h_done, n - 1)
                if n - 2 >= HT * SPLIT_FROM:
                    pe.wait_ge(h_hi_done, n - 1 - HT * SPLIT_FROM)
                col = slice(c * P, (c + 1) * P)
                three(H_PS[n % 2][:], w1_hi[:, b % 2, j, col], w1_lo[:, b % 2, j, col],
                      xT_hi[:, b], xT_lo[:, b]).then_inc(h_ps, 1)

            def expert_out(n):
                b, i = n // HT, n % HT
                if i == 0:
                    pe.wait_ge(w2_scaled, b + 1)
                    if b >= 1:
                        pe.wait_ge(yT_done, b)
                pe.wait_ge(h_done, n + 1)
                j, c = i // FC, i % FC
                if b < SPLIT_FROM:
                    nc.tensor.matmul(OUT_PS[:], w2_s[:, b % 2, j, c], h_ring[:, n % NH],
                                     start=(i == 0), stop=(i == HT - 1)).then_inc(w2_mm, 1)
                else:
                    pe.wait_ge(h_split, n - HT * SPLIT_FROM + 1)
                    three(OUT_PS[:], w2_hi[:, b % 2, j, c], w2_lo[:, b % 2, j, c],
                          h_hi[:, n % NH], h_lo[:, n % NH],
                          start=(i == 0), stop=(i == HT - 1)).then_inc(w2_mm, 1)

            def transform(q):
                kc = q % KC
                if q == 0:
                    pe.wait_ge(cs_split, 1)
                    pe.wait_ge(A_done, 2)
                if kc == 0:
                    pe.wait_ge(pm_split, GB * (q // KC + 1))
                for ri, (done, read) in enumerate(((vre_ps, vre_read), (vim_ps, vim_read))):
                    if q >= 1:
                        pe.wait_ge(read, q)
                    for c in range(NC):
                        col = slice(kc * P, (kc + 1) * P)
                        last = three(V_RI[ri][:], cs_hi[:, c, ri, col], cs_lo[:, c, ri, col],
                                     pm_hi[:, ri, c].rearrange("p b d -> p (b d)"),
                                     pm_lo[:, ri, c].rearrange("p b d -> p (b d)"),
                                     start=(c == 0), stop=(c == NC - 1))
                    last.then_inc(done, 1)

            def transform_back(b, parts=(0, 1)):
                pe.wait_ge(Y_done, KC * (b // GB + 1))
                if b == 0:
                    pe.wait_ge(inv_in, 16)
                if b >= 1:
                    pe.wait_ge(eo_read, b)
                for ri in parts:
                    for kc in range(KC):
                        last = nc.tensor.matmul(EO_PS[:, ri * S // 2:(ri + 1) * S // 2],
                                                Y[:, kc, ri, b % GB], inv_sb[:, kc, ri],
                                                start=(kc == 0), stop=(kc == KC - 1))
                if parts[-1] == 1:
                    last.then_inc(eo_ps, 1)

            def transpose_y(b):
                pe.wait_ge(yT_done, b + 1)
                if b >= 1:
                    pe.wait_ge(y_read, b)
                for t in range(NT):
                    last = nc.tensor.transpose(YT_PS[:, t * P:(t + 1) * P],
                                               yT[:, b % NY, t * P:(t + 1) * P], ident)
                last.then_inc(y_ps, 1)

            def mixed(b):
                pe.wait_ge(conv_done, b + 1)
                if b == 0:
                    pe.wait_ge(last_in, 16 * 3)
                if b >= 1:
                    pe.wait_ge(s_read, b)
                for t in range(NT):
                    last = nc.tensor.matmul(S_PS[:, t * P:(t + 1) * P], uT[:, b, t * P:(t + 1) * P],
                                            ow_sb[:], start=True, stop=True)
                last.then_inc(s_ps, 1)

            pe.wait_ge(sel_done, 1)
            pe.wait_ge(v_done, B)
            hidden(0)
            hidden(1)
            for n in range(HT * B):
                if n + 2 < HT * B:
                    hidden(n + 2)
                expert_out(n)
                if n == PRODUCT_AT:
                    layer_product(L)
                if n == VARIANCE_AT:
                    layer_variance(L)
                if n == ROOT_AT:
                    layer_root_back(L)
                if n == LAGS_AT:
                    even_odd_lags()
                for kc in (kc for kc in range(KC) if SPECTRUM_AT[kc] == n):
                    filter_spectrum(kc)
                if n in FORTH_AT:
                    transform(FORTH_AT.index(n))
                if n in YT_AT:
                    transpose_y(YT_AT.index(n))
                if n in BACK_AT and n < HT * B - 1:
                    transform_back(BACK_AT.index(n))
                if n in S_AT and n < HT * B - 1:
                    mixed(S_AT.index(n))
            transform_back(B - 1, (0,))
            transpose_y(B - 1)
            transform_back(B - 1, (1,))
            mixed(B - 1)


NAMES = ["L0_attn_x", "L0_attn_uv_w", "L0_attn_o_w", "L0_attn_rpe_pos_w", "L0_attn_rpe_ln_w",
         "L0_attn_rpe_ln_b", "L0_attn_rpe_fc_w", "L0_attn_rpe_out_ln_w", "L0_attn_rpe_out_ln_b",
         "L0_attn_rpe_out_w", "L0_ffn_W1", "L0_ffn_b1", "L0_ffn_W2", "L0_ffn_b2", "L0_ffn_Wr",
         "L0_ffn_br", "L0_ffn_gamma", "L0_ffn_beta"]


def kernel(**inputs):
    import concourse.bacc as bacc
    from concourse.bass_utils import run_bass_kernel_spmd

    nc = bacc.Bacc("TRN2", target_bir_lowering=False, num_devices=1)
    arrays = {f"in_{n}": np.ascontiguousarray(inputs[n]) for n in NAMES}
    arrays.update({f"table_{n}": a for n, a in shape_tables().items()})
    args = [nc.dram_tensor(n, a.shape, mybir.dt.from_np(a.dtype), kind="ExternalInput").ap()
            for n, a in arrays.items()]
    args.append(nc.dram_tensor("out_0_dram", (B, S, D), F32, kind="ExternalOutput").ap())
    build(nc, *args)
    r = run_bass_kernel_spmd(nc, [arrays], core_ids=[0])
    return r.results[0]["out_0_dram"]
```
